# Optimizing a Trainium2 kernel written in Bass

```python
import numpy as np
import jax
import jax.numpy as jnp

def _softmax(x, axis=-1):
    return jax.nn.softmax(x, axis=axis)

def _gelu(x):
    return jax.nn.gelu(x, approximate=True)

def _silu(x):
    return jax.nn.silu(x)

def _sigmoid(x):
    return jax.nn.sigmoid(x)

def _layernorm(x, axis=-1, eps=1e-05):
    m = jnp.mean(x, axis=axis, keepdims=True)
    v = jnp.var(x, axis=axis, keepdims=True)
    return (x - m) / jnp.sqrt(v + eps)

def _scatter_add(tgt, idx, src, axis=0):
    return tgt.at[idx].add(src)

def _segment_sum(src, seg, n):
    return jax.ops.segment_sum(src, seg, n)
kernel_name = 'mk_adj_resnorm_d4_adj_r2_a10181'

def setup_inputs(seed: int=0):
    np.random.seed(seed)
    _w = jnp.asarray

    def _rec_inputs():
        import jax
        import jax.numpy as jnp
        _gk = jax.random.key(seed)
        x = -0.0001546 + 1 * jax.random.normal(jax.random.fold_in(_gk, 1), (128, 128, 128), jnp.float32)
        _w = (1.0 + jnp.arange(128, dtype=jnp.float32)) ** (-0.5)
        _w = _w / _w.mean()
        _pij = jnp.clip(0.03125 * _w[:, None] * _w[None, :], 0.0, 1.0)
        _a = jax.random.uniform(jax.random.fold_in(_gk, 2), (128, 128)) < _pij
        _a = jnp.logical_or(_a, jnp.swapaxes(_a, -1, -2))
        _a = jnp.logical_or(_a, jnp.eye(128, dtype=bool))
        _af = _a.astype(jnp.float32)
        _af = _af * jax.random.uniform(jax.random.fold_in(_gk, 3), (128, 128), jnp.float32, 0.05, 0.999927)
        adj = _af
        return (x, adj)
    x, adj = _rec_inputs()

    def _L0_gnn_setup():
        import jax, jax.numpy as jnp
        import numpy as np
        B, N, D = (2048, 128, 128)
        key = jax.random.key(seed)
        ks = jax.random.split(key, 6)
        return {'label': jax.random.normal(ks[0], (B, N, D), dtype=jnp.float32), 'adj_in': jax.random.uniform(ks[1], (N, N), dtype=jnp.float32), 'adj_out': jax.random.uniform(ks[2], (N, N), dtype=jnp.float32), 'edge_bias': jnp.zeros((N, D), dtype=jnp.float32), 'gate_weight': jax.random.normal(ks[3], (D, 1), dtype=jnp.float32) * (6.0 / (D + 1)) ** 0.5, 'bias_gate': jnp.zeros((N, 1), dtype=jnp.float32), 'out_edge_bias': jnp.zeros((N, D), dtype=jnp.float32), 'out_gate_weight': jax.random.normal(ks[4], (D, 1), dtype=jnp.float32) * (6.0 / (D + 1)) ** 0.5, 'out_bias_gate': jnp.zeros((N, 1), dtype=jnp.float32), 'loop_gate': jax.random.normal(ks[5], (D, 1), dtype=jnp.float32) * (6.0 / (D + 1)) ** 0.5}
    _L0_gnn_all = _L0_gnn_setup()
    _L0_gnn_in = {k: v for k, v in _L0_gnn_all.items() if k in ('edge_bias', 'gate_weight', 'bias_gate', 'out_edge_bias', 'out_gate_weight', 'out_bias_gate', 'loop_gate')}
    del _L0_gnn_all

    def _L1_gnn_setup():
        import jax, jax.numpy as jnp
        import numpy as np
        B, T, D, H = (64, 1024, 128, 128)
        MAX_SKIP = 4

        def _lstm_last(Wih, Whh, bih, bhh, xs):
            N, _, Hd = xs.shape
            bias = bih + bhh

            def step(carry, x_t):
                h, c = carry
                g = x_t @ Wih.T + h @ Whh.T + bias
                i, f, gg, o = jnp.split(g, 4, axis=-1)
                c = jax.nn.sigmoid(f) * c + jax.nn.sigmoid(i) * jnp.tanh(gg)
                h = jax.nn.sigmoid(o) * jnp.tanh(c)
                return ((h, c), None)
            init = (jnp.zeros((N, Hd), xs.dtype), jnp.zeros((N, Hd), xs.dtype))
            (h_last, _), _ = jax.lax.scan(step, init, jnp.swapaxes(xs, 0, 1))
            return h_last
        key = jax.random.key(seed)
        ks = jax.random.split(key, 8)
        s = 0.05
        x = jax.random.normal(ks[0], (B, T, D), jnp.float32)
        adj = jax.random.uniform(ks[1], (T, T), jnp.float32) / T
        Wg0 = jax.random.normal(ks[2], (D, H), jnp.float32) * s
        bg0 = jnp.zeros((H,), jnp.float32)
        Wg1 = jax.random.normal(ks[3], (H, H), jnp.float32) * s
        bg1 = jnp.zeros((H,), jnp.float32)
        Wih = jax.random.normal(ks[4], (MAX_SKIP, 4 * H, H), jnp.float32) * s
        Whh = jax.random.normal(ks[5], (MAX_SKIP, 4 * H, H), jnp.float32) * s
        bih = jax.random.normal(ks[6], (MAX_SKIP, 4 * H), jnp.float32) * s
        bhh = jax.random.normal(ks[7], (MAX_SKIP, 4 * H), jnp.float32) * s
        return dict(x=x, adj=adj, Wg0=Wg0, bg0=bg0, Wg1=Wg1, bg1=bg1, Wih=Wih, Whh=Whh, bih=bih, bhh=bhh)
    _L1_gnn_all = _L1_gnn_setup()
    _L1_gnn_in = {k: v for k, v in _L1_gnn_all.items() if k in ('Wg0', 'bg0', 'Wg1', 'bg1', 'Wih', 'Whh', 'bih', 'bhh')}
    del _L1_gnn_all

    def _L2_gnn_setup():
        import jax, jax.numpy as jnp
        import numpy as np
        EPS = 1e-05

        def _batchnorm(x, gamma, beta):
            mu = jnp.mean(x, axis=0)
            var = jnp.var(x, axis=0)
            return (x - mu) * jax.lax.rsqrt(var + EPS) * gamma + beta
        key = jax.random.key(seed)
        ks = jax.random.split(key, 4)
        b, n, d, h, o = (32, 1024, 128, 256, 128)
        features = jax.random.normal(ks[0], (b, n, d), dtype=jnp.float32)
        A = jax.random.uniform(ks[1], (n, n), dtype=jnp.float32)
        lim1 = float(np.sqrt(6.0 / (d + h)))
        W1 = jax.random.uniform(ks[2], (h, d), minval=-lim1, maxval=lim1, dtype=jnp.float32)
        b1 = jnp.zeros((h,), jnp.float32)
        lim2 = float(np.sqrt(6.0 / (h + o)))
        W2 = jax.random.uniform(ks[3], (o, h), minval=-lim2, maxval=lim2, dtype=jnp.float32)
        b2 = jnp.zeros((o,), jnp.float32)
        g1 = jnp.ones((h,), jnp.float32)
        be1 = jnp.zeros((h,), jnp.float32)
        g2 = jnp.ones((o,), jnp.float32)
        be2 = jnp.zeros((o,), jnp.float32)
        return {'features': features, 'A': A, 'W1': W1, 'b1': b1, 'g1': g1, 'be1': be1, 'W2': W2, 'b2': b2, 'g2': g2, 'be2': be2}
    _L2_gnn_all = _L2_gnn_setup()
    _L2_gnn_in = {k: v for k, v in _L2_gnn_all.items() if k in ('W1', 'b1', 'g1', 'be1', 'W2', 'b2', 'g2', 'be2')}
    del _L2_gnn_all

    def _L3_gnn_setup():
        import jax, jax.numpy as jnp
        import numpy as np
        B, N, IN_DIM, OUT_DIM, H = (2, 2048, 128, 128, 4)
        HEAD_DIM = OUT_DIM // H
        EDGE_P = 0.01
        key = jax.random.key(seed)
        k1, k2, k3 = jax.random.split(key, 3)
        h = jax.random.normal(k1, (B, N, IN_DIM), dtype=jnp.float32)
        W = jax.random.normal(k2, (IN_DIM, 3 * OUT_DIM), dtype=jnp.float32) / np.sqrt(IN_DIM)
        adj = (jax.random.uniform(k3, (N, N)) < EDGE_P).astype(jnp.float32)
        adj = jnp.maximum(adj, jnp.eye(N, dtype=jnp.float32))
        return {'h': h, 'W': W, 'adj': adj}
    _L3_gnn_all = _L3_gnn_setup()
    _L3_gnn_in = {k: v for k, v in _L3_gnn_all.items() if k in ('W',)}
    del _L3_gnn_all
    return {'x': x, 'adj': adj, 'L0_gnn_edge_bias': _L0_gnn_in['edge_bias'], 'L0_gnn_gate_weight': _L0_gnn_in['gate_weight'], 'L0_gnn_bias_gate': _L0_gnn_in['bias_gate'], 'L0_gnn_out_edge_bias': _L0_gnn_in['out_edge_bias'], 'L0_gnn_out_gate_weight': _L0_gnn_in['out_gate_weight'], 'L0_gnn_out_bias_gate': _L0_gnn_in['out_bias_gate'], 'L0_gnn_loop_gate': _L0_gnn_in['loop_gate'], 'L1_gnn_Wg0': _L1_gnn_in['Wg0'], 'L1_gnn_bg0': _L1_gnn_in['bg0'], 'L1_gnn_Wg1': _L1_gnn_in['Wg1'], 'L1_gnn_bg1': _L1_gnn_in['bg1'], 'L1_gnn_Wih': _L1_gnn_in['Wih'], 'L1_gnn_Whh': _L1_gnn_in['Whh'], 'L1_gnn_bih': _L1_gnn_in['bih'], 'L1_gnn_bhh': _L1_gnn_in['bhh'], 'L2_gnn_W1': _L2_gnn_in['W1'], 'L2_gnn_b1': _L2_gnn_in['b1'], 'L2_gnn_g1': _L2_gnn_in['g1'], 'L2_gnn_be1': _L2_gnn_in['be1'], 'L2_gnn_W2': _L2_gnn_in['W2'], 'L2_gnn_b2': _L2_gnn_in['b2'], 'L2_gnn_g2': _L2_gnn_in['g2'], 'L2_gnn_be2': _L2_gnn_in['be2'], 'L3_gnn_W': _L3_gnn_in['W']}

def reference(x, adj, L0_gnn_edge_bias, L0_gnn_gate_weight, L0_gnn_bias_gate, L0_gnn_out_edge_bias, L0_gnn_out_gate_weight, L0_gnn_out_bias_gate, L0_gnn_loop_gate, L1_gnn_Wg0, L1_gnn_bg0, L1_gnn_Wg1, L1_gnn_bg1, L1_gnn_Wih, L1_gnn_Whh, L1_gnn_bih, L1_gnn_bhh, L2_gnn_W1, L2_gnn_b1, L2_gnn_g1, L2_gnn_be1, L2_gnn_W2, L2_gnn_b2, L2_gnn_g2, L2_gnn_be2, L3_gnn_W):
    import jax
    import jax.numpy as jnp

    def _L0_gnn_ref(label, adj_in, adj_out, edge_bias, gate_weight, bias_gate, out_edge_bias, out_gate_weight, out_bias_gate, loop_gate):
        import jax, jax.numpy as jnp
        import numpy as np
        B, N, D = (2048, 128, 128)
        h = label
        origin = jax.lax.stop_gradient(jnp.where(adj_in <= 0, adj_in, 1.0))
        h_in = jnp.einsum('mn,bnd->bmd', origin * adj_in, h)
        in_gate = jnp.einsum('bnd,do->bno', h, gate_weight) + bias_gate
        msg_in = (h_in + edge_bias) * jax.nn.sigmoid(in_gate)
        h_out = jnp.einsum('mn,bnd->bmd', origin.T * adj_out, h)
        out_gate = jnp.einsum('bnd,do->bno', h, out_gate_weight) + out_bias_gate
        msg_out = (h_out + out_edge_bias) * jax.nn.sigmoid(out_gate)
        lp_gate = jnp.einsum('bnd,do->bno', h, loop_gate)
        msg_loop = h * jax.nn.sigmoid(lp_gate)
        return jax.nn.relu(msg_in + msg_out + msg_loop)

    def _L1_gnn_ref(x, adj, Wg0, bg0, Wg1, bg1, Wih, Whh, bih, bhh):
        import jax, jax.numpy as jnp
        import numpy as np
        B, T, D, H = (64, 1024, 128, 128)
        MAX_SKIP = 4

        def _lstm_last(Wih, Whh, bih, bhh, xs):
            N, _, Hd = xs.shape
            bias = bih + bhh

            def step(carry, x_t):
                h, c = carry
                g = x_t @ Wih.T + h @ Whh.T + bias
                i, f, gg, o = jnp.split(g, 4, axis=-1)
                c = jax.nn.sigmoid(f) * c + jax.nn.sigmoid(i) * jnp.tanh(gg)
                h = jax.nn.sigmoid(o) * jnp.tanh(c)
                return ((h, c), None)
            init = (jnp.zeros((N, Hd), xs.dtype), jnp.zeros((N, Hd), xs.dtype))
            (h_last, _), _ = jax.lax.scan(step, init, jnp.swapaxes(xs, 0, 1))
            return h_last
        h = jax.nn.relu(jnp.einsum('ts,bsh->bth', adj, x @ Wg0 + bg0))
        h = jax.nn.relu(jnp.einsum('ts,bsh->bth', adj, h @ Wg1 + bg1))
        Bv, Tv, Hd = h.shape
        for p in range(1, MAX_SKIP + 1):
            nw = Tv // p
            wins = h[:, :nw * p, :].reshape(Bv * nw, p, Hd)
            last = _lstm_last(Wih[p - 1], Whh[p - 1], bih[p - 1], bhh[p - 1], wins)
            idx = jnp.arange(nw) * p + (p - 1)
            h = h.at[:, idx, :].set(last.reshape(Bv, nw, Hd))
        return h

    def _L2_gnn_ref(features, A, W1, b1, g1, be1, W2, b2, g2, be2):
        import jax, jax.numpy as jnp
        import numpy as np
        EPS = 1e-05

        def _batchnorm(x, gamma, beta):
            mu = jnp.mean(x, axis=0)
            var = jnp.var(x, axis=0)
            return (x - mu) * jax.lax.rsqrt(var + EPS) * gamma + beta
        b, n, d = features.shape
        A_norm = A + jnp.eye(n, dtype=A.dtype)
        deg = jnp.sum(A_norm, axis=0) + jnp.sum(A_norm, axis=1) - jnp.diagonal(A_norm)
        dinv = jax.lax.rsqrt(deg)
        A_hat = A_norm * dinv[:, None] * dinv[None, :]
        agg = jnp.einsum('nm,bmd->bnd', A_hat, features)
        x = agg.reshape(-1, d)
        h = jax.nn.relu(_batchnorm(x @ W1.T + b1, g1, be1))
        out = h @ W2.T + b2
        out = _batchnorm(out, g2, be2)
        return out.reshape(b, n, -1)

    def _L3_gnn_ref(h, W, adj):
        import jax, jax.numpy as jnp
        import numpy as np
        B, N, IN_DIM, OUT_DIM, H = (2, 2048, 128, 128, 4)
        HEAD_DIM = OUT_DIM // H
        EDGE_P = 0.01
        Bn, Nn, _ = h.shape
        qkv = h @ W
        qkv = qkv.reshape(Bn, Nn, 3, H, HEAD_DIM).transpose(2, 0, 3, 1, 4)
        q, k, v = (qkv[0], qkv[1], qkv[2])
        mask = jnp.where(adj == 0, -jnp.inf, 0.0)
        scores = jnp.einsum('bhid,bhjd->bhij', q, k) / np.sqrt(HEAD_DIM) + mask
        attn = jax.nn.softmax(scores, axis=-1)
        out = jnp.einsum('bhij,bhjd->bhid', attn, v)
        return out.transpose(0, 2, 1, 3).reshape(Bn, Nn, OUT_DIM)
    x = _layernorm(x + _L0_gnn_ref(x, adj, adj, L0_gnn_edge_bias, L0_gnn_gate_weight, L0_gnn_bias_gate, L0_gnn_out_edge_bias, L0_gnn_out_gate_weight, L0_gnn_out_bias_gate, L0_gnn_loop_gate), axis=-1)
    x = _layernorm(x + _L1_gnn_ref(x, adj, L1_gnn_Wg0, L1_gnn_bg0, L1_gnn_Wg1, L1_gnn_bg1, L1_gnn_Wih, L1_gnn_Whh, L1_gnn_bih, L1_gnn_bhh), axis=-1)
    x = _layernorm(x + _L2_gnn_ref(x, adj, L2_gnn_W1, L2_gnn_b1, L2_gnn_g1, L2_gnn_be1, L2_gnn_W2, L2_gnn_b2, L2_gnn_g2, L2_gnn_be2), axis=-1)
    x = _layernorm(x + _L3_gnn_ref(x, L3_gnn_W, adj), axis=-1)
    return x

_drawn_inputs = setup_inputs


def setup_inputs(seed=0):
    import zlib

    import numpy as np

    out = dict(_drawn_inputs(seed))
    spreads = {'L0_gnn_edge_bias': (0.0, 0.359),
     'L0_gnn_bias_gate': (0.0, 0.8),
     'L0_gnn_out_edge_bias': (0.0, 0.356),
     'L0_gnn_out_bias_gate': (0.0, 0.8),
     'L1_gnn_bg0': (0.0, 0.1),
     'L1_gnn_bg1': (0.0, 0.303),
     'L2_gnn_b1': (0.0, 0.8),
     'L2_gnn_g1': (1.0, 0.2),
     'L2_gnn_be1': (0.0, 0.1),
     'L2_gnn_b2': (0.0, 0.8),
     'L2_gnn_g2': (1.0, 0.2),
     'L2_gnn_be2': (0.0, 0.1)}
    factors = {'L1_gnn_Whh': 8.0, 'L1_gnn_bih': 2.907, 'L1_gnn_bhh': 2.981}
    for name, (base, spread) in spreads.items():
        noise = np.random.default_rng([zlib.crc32(name.encode()), seed]).standard_normal(out[name].shape)
        drawn = base * np.exp(spread * noise) if base else spread * noise
        out[name] = jnp.asarray(drawn.astype(out[name].dtype))
    for name, factor in factors.items():
        out[name] = (out[name] * factor).astype(out[name].dtype)
    return out
```

```python
from contextlib import ExitStack

import concourse.bass as bass
from concourse import mybir

F32 = mybir.dt.float32
ALU = mybir.AluOpType
ACT = mybir.ActivationFunctionType
AX = mybir.AxisListType.X

B, N, D = 128, 128, 128
GB = 4
S = 2
NIT = B // (GB * S)
NG = B // GB
C = GB * N
H1 = 2
NH, HD = 4, 32
EPS = 1e-5
MASKED = -3.0e38
MAXW = 4
GI, GF, GG, GO = range(4)


class Steps:

    def __init__(self, *names):
        self.at = {n: k + 1 for k, n in enumerate(names)}
        self.total = len(names)

    def done(self, it, name):
        return it * self.total + (self.total + self.at[name])

    def done_before(self, it, name):
        return it * self.total + self.at[name]


UNITS = [(1, 0, N, 0, GB // 2), (1, 0, N, GB // 2, GB // 2)]
UNITS += [(p, j, N // p, 0, GB) for p in range(2, MAXW + 1) for j in range(p)]
NU = len(UNITS)

PRE_PE = Steps("gates", "in", "out", "x1t", "xw0", "ax0", "xw1", "ax1")
PRE_DVE = Steps("gates", "in", "out", "loop", "acc_in", "acc_out", "y", "stats", "aggr", "x1", "xw0", "xw1")
PRE_ACT = Steps("gates", "x1t", "h1", "h2")
PRE_POOL = Steps("veps", "rstd")
CELL_PE = Steps(*[f"{u}{x}" for u in range(NU) for x in ("ig", "fo")])
CELL_ACT = Steps(*[f"{u}{x}" for u in range(NU) for x in (("i", "g", "o", "t") if UNITS[u][1] == 0 else ("i", "g", "f", "o", "t"))])
CELL_DVE = Steps(*[f"{u}{x}" for u in range(NU) for x in (("c", "h") if UNITS[u][1] == 0 else ("ig", "fc", "c", "h"))])
POST_PE = Steps("hT", "agg", "w1a", "w1b")
POST_DVE = Steps("y", "stats", "aggr", "x2", "bna", "bnb")
POST_ACT = Steps("agg")
POST_POOL = Steps("veps", "rstd")

MLP_PE = Steps("w1a", "w1b", "w2")
MLP_ACT = Steps("h0", "h1", "out")
MLP_DVE = Steps("bn")

ATT_PE = Steps("zt", "x3t", "q", "k", "v", "sc0", "sc1", "pt0", "sc2", "pt1", "sc3", "pv0", "pt2", "pv1", "pt3", "pv2", "pv3")
ATT_ACT = Steps("z", "x3t", "q", "v", "exp0", "exp1", "pt0", "exp2", "pt1", "exp3", "pt2", "pt3")
ATT_DVE = Steps("y", "stats", "aggr", "x3", "k", "m0", "max0", "m1", "max1", "m2", "max2", "m3", "max3",
                "rec", "att", "y3", "stats3", "aggr3", "out")
ATT_POOL = Steps("veps", "rstd", "sub0", "sub1", "sub2", "sub3", "veps3", "rstd3")


def build(nc, t, out):
    x2_dram = nc.dram_tensor("x2_dram", (N, B, D), F32, kind="Internal").ap()

    with ExitStack() as top:
        def sb(name, shape, ctx=top):
            return ctx.enter_context(nc.sbuf_tensor(name, shape, F32))

        def sem(name, ctx=top):
            return ctx.enter_context(nc.semaphore(name))

        def flat(ap):
            return ap.rearrange("p a b -> p (a b)")

        bank = [top.enter_context(nc.psum_tensor(f"bank{k}", [128, 512], F32)) for k in range(8)]
        tile = [b[:].rearrange("p (g c) -> p g c", g=GB) for b in bank]

        agg_all = sb("agg_all", [128, B, N])
        ident = sb("ident", [128, 128])
        minus_half = sb("minus_half", [128, GB])
        w1T = sb("w1T", [128, H1 * 128])
        w2T = sb("w2T", [128, H1, 128])
        w3 = sb("w3", [128, 3 * D])
        mask = sb("mask", [128, 128])
        bn1_stats = sb("bn1_stats", [128, H1, NG, 6])
        bn2_stats = sb("bn2_stats", [128, NG, 6])
        bn1_par = sb("bn1_par", [128, 3, H1])
        bn2_par = sb("bn2_par", [128, 3])
        carrier = sem("carrier")
        consts_in = sem("consts_in")

        def settle(eng):
            eng.sem_inc(carrier, 1)

        with ExitStack() as one:
            def sb1(name, shape):
                return sb(name, shape, one)

            adj, adjT = sb1("adj", [128, 128]), sb1("adjT", [128, 128])
            w_inT, w_outT = sb1("w_inT", [128, 128]), sb1("w_outT", [128, 128])
            a_hatT = sb1("a_hatT", [128, 128])
            eb, oeb = sb1("eb", [128, 128]), sb1("oeb", [128, 128])
            gate_w, gate_b = sb1("gate_w", [128, 3]), sb1("gate_b", [128, 3])
            wg0, wg1 = sb1("wg0", [128, 128]), sb1("wg1", [128, 128])
            bg0, bg1 = sb1("bg0", [128, 128]), sb1("bg1", [128, 128])
            wihT, whhT = sb1("wihT", [128, MAXW, 512]), sb1("whhT", [128, MAXW, 512])
            bih, bhh, b_cell = (sb1(n, [128, MAXW * 4]) for n in ("bih", "bhh", "b_cell"))
            deg = sb1("deg", [128, 8])

            x_t = [sb1(f"x_t{s}", [128, GB, D]) for s in range(S)]
            x_f = [sb1(f"x_f{s}", [128, GB, N]) for s in range(S)]
            u_in, u_out = sb1("u_in", [128, GB, D]), sb1("u_out", [128, GB, D])
            gz, sg = ([sb1(f"{n}{s}", [128, GB, 3]) for s in range(S)] for n in ("gz", "sg"))
            y1 = [sb1(f"y1_{s}", [128, GB, D]) for s in range(S)]
            x1 = [sb1(f"x1_{s}", [128, GB, D]) for s in range(S)]
            x1T, xw, h1T = sb1("x1T", [128, GB, D]), sb1("xw", [128, GB, D]), sb1("h1T", [128, GB, D])
            hT = [sb1(f"hT{s}", [128, GB, N]) for s in range(S)]
            seq = [sb1(f"seq{s}", [128, GB, N]) for s in range(S)]
            hid = [sb1(f"hid{s}", [128, 256]) for s in range(S)]
            gi, gf, gg, go, ct, cc, ig = ([sb1(f"{n}{s}", [128, 256]) for s in range(S)]
                                          for n in ("gi", "gf", "gg", "go", "ct", "cc", "ig"))
            y2 = [sb1(f"y2_{s}", [128, GB, D]) for s in range(S)]
            x2 = [sb1(f"x2_{s}", [128, GB, D]) for s in range(S)]
            agg = [sb1(f"agg{s}", [128, GB, N]) for s in range(S)]
            ln_s = [sb1(f"ln_s{s}", [128, GB, 6]) for s in range(S)]
            ln_mv = [sb1(f"ln_mv{s}", [128, GB, 2]) for s in range(S)]
            ln_r = [sb1(f"ln_r{s}", [128, GB]) for s in range(S)]
            post_s = [sb1(f"post_s{s}", [128, GB, 6]) for s in range(S)]
            post_mv = [sb1(f"post_mv{s}", [128, GB, 2]) for s in range(S)]
            post_r = [sb1(f"post_r{s}", [128, GB]) for s in range(S)]

            with ExitStack() as zero:
                pool_set, dve_set, dve_link, pe_set = (sem(n, zero) for n in ("pool_set", "dve_set", "dve_link", "pe_set"))
                tmp, tmp2, origin, an = (sb(n, [128, 128], zero) for n in ("tmp", "tmp2", "origin", "an"))
                with nc.Block() as block:
                    loads = [(adj, t["adj"]), (adjT, t["adjT"]), (eb, t["eb"]), (oeb, t["oeb"]), (gate_w, t["gate_w"]),
                             (wg0, t["wg0"]), (wg1, t["wg1"]), (bg0, t["bg0"].partition_broadcast(128)),
                             (bg1, t["bg1"].partition_broadcast(128)), (wihT, t["wihT"]), (whhT, t["whhT"]),
                             (bih, t["bih"]), (bhh, t["bhh"]), (w1T, t["w1T"]), (w2T, t["w2T"]), (w3, t["w3"]),
                             (bn1_par, t["bn1"]), (bn2_par, t["bn2"])]

                    @block.sync
                    def _(sp):
                        for dst, src in loads:
                            sp.dma_start(dst[:], src).then_inc(consts_in, 16)
                        sp.dma_start(gate_b[:, 0:2], t["gate_b"]).then_inc(consts_in, 16)
                        sp.wait_ge(consts_in, 16 * (len(loads) + 1))

                    @block.gpsimd
                    def _(pool):
                        pool.memset(ident[:], 0.0).then_inc(pool_set, 1)
                        pool.memset(minus_half[:], -0.5).then_inc(pool_set, 1)
                        pool.wait_ge(pool_set, 2)
                        pool.affine_select(out=ident[:], in_=ident[:], compare_op=ALU.not_equal, fill=1.0, base=0,
                                           pattern=[[-1, 128]], channel_multiplier=1).then_inc(pool_set, 1)
                        pool.memset(gate_b[:, 2:3], 0.0).then_inc(pool_set, 1)
                        pool.wait_ge(dve_set, 11)
                        pool.tensor_tensor(deg[:, 4:5], deg[:, 3:4], minus_half[:, 0:1], ALU.pow).then_inc(pool_set, 1)

                    @block.vector
                    def _(dve):
                        done = [0]

                        def step(ins):
                            done[0] += 1
                            ins.then_inc(dve_set, 1)
                            dve.wait_ge(dve_set, done[0])

                        dve.wait_ge(consts_in, 16 * (len(loads) + 1))
                        dve.wait_ge(pool_set, 3)
                        step(nc.vector.tensor_scalar(tmp[:], adjT[:], 0.0, None, ALU.is_gt))
                        step(nc.vector.scalar_tensor_tensor(tmp2[:], adjT[:], 0.0, tmp[:], ALU.min, ALU.add))
                        step(nc.vector.tensor_tensor(w_inT[:], tmp2[:], adjT[:], ALU.mult))
                        step(nc.vector.tensor_scalar(tmp[:], adj[:], 0.0, None, ALU.is_gt))
                        step(nc.vector.scalar_tensor_tensor(origin[:], adj[:], 0.0, tmp[:], ALU.min, ALU.add))
                        step(nc.vector.tensor_tensor(w_outT[:], origin[:], adjT[:], ALU.mult))
                        step(nc.vector.tensor_tensor(an[:], adj[:], ident[:], ALU.add))
                        step(nc.vector.reduce_sum(deg[:, 0:1], an[:], AX))
                        step(nc.vector.tensor_tensor(tmp[:], adjT[:], ident[:], ALU.add))
                        step(nc.vector.tensor_tensor(tmp2[:], ident[:], an[:], ALU.mult))
                        nc.vector.reduce_sum(deg[:, 1:2], tmp[:], AX)
                        nc.vector.reduce_sum(deg[:, 2:3], tmp2[:], AX).then_inc(dve_link, 1)
                        dve.wait_ge(dve_link, 1)
                        nc.vector.tensor_tensor(deg[:, 5:6], deg[:, 1:2], deg[:, 2:3], ALU.subtract).then_inc(dve_link, 1)
                        dve.wait_ge(dve_link, 2)
                        step(nc.vector.tensor_tensor(deg[:, 3:4], deg[:, 0:1], deg[:, 5:6], ALU.add))
                        step(nc.vector.tensor_scalar(mask[:], adj[:], 0.0, MASKED, ALU.is_equal, ALU.mult))
                        step(nc.vector.tensor_tensor(b_cell[:], bih[:], bhh[:], ALU.add))
                        dve.wait_ge(pool_set, 5)
                        step(nc.vector.tensor_scalar(tmp[:], ident[:], deg[:, 4:5], None, ALU.mult))
                        dve.wait_ge(pe_set, 1)
                        step(nc.vector.tensor_scalar(a_hatT[:], bank[0][:, 0:128], deg[:, 4:5], None, ALU.mult))

                    @block.tensor
                    def _(pe):
                        pe.wait_ge(dve_set, 14)
                        pe.matmul(bank[0][:, 0:128], an[:], tmp[:], start=True, stop=True).then_inc(pe_set, 1)

            x_in = [sem(f"x_in{s}", one) for s in range(S)]
            x2_out = [sem(f"x2_out{s}", one) for s in range(S)]
            agg_out = [sem(f"agg_out{s}", one) for s in range(S)]
            pre_pe, pre_act, pre_dve, pre_pool, cell_pe, cell_act, cell_dve, post_pe, post_act, post_dve, post_pool = (
                [sem(f"{n}{s}", one) for s in range(S)]
                for n in ("pre_pe", "pre_act", "pre_dve", "pre_pool", "cell_pe", "cell_act", "cell_dve",
                          "post_pe", "post_act", "post_dve", "post_pool"))
            PB = [bank[0], bank[1]]
            QB = [bank[2], bank[3]]
            PT, QT = [tile[0], tile[1]], [tile[2], tile[3]]
            GATE = [[bank[4], bank[5]], [bank[6], bank[7]]]

            def group(it, s):
                return bass.ds(it * (S * GB) + s * GB, GB)

            with nc.Block() as block:
                @block.sync
                def _(sp):
                    for s in range(S):
                        sp.sem_inc(x2_out[s], 16)
                        sp.sem_inc(agg_out[s], 16)
                    with sp.Fori(0, NIT) as it:
                        for s in range(S):
                            sp.wait_ge(pre_dve[s], PRE_DVE.done_before(it, "y"))
                            settle(sp)
                            sp.wait_ge(pre_pe[s], PRE_PE.done_before(it, "gates"))
                            settle(sp)
                            sp.dma_start(x_t[s][:], t["x_t"][:, group(it, s), :]).then_inc(x_in[s], 16)
                            sp.dma_start(x_f[s][:], t["x_f"][:, group(it, s), :]).then_inc(x_in[s], 16)
                        for s in range(S):
                            sp.wait_ge(post_act[s], POST_ACT.done(it, "agg"))
                            settle(sp)
                            sp.dma_start(agg_all[:, group(it, s), :], agg[s][:]).then_inc(agg_out[s], 16)
                            sp.wait_ge(post_dve[s], POST_DVE.done(it, "x2"))
                            settle(sp)
                            sp.dma_start(x2_dram[:, group(it, s), :], x2[s][:]).then_inc(x2_out[s], 16)
                    for s in range(S):
                        sp.wait_ge(agg_out[s], 16 * NIT + 16)
                        sp.wait_ge(x2_out[s], 16 * NIT + 16)

                @block.tensor
                def _(pe):
                    for s in range(S):
                        pe.sem_inc(pre_pe[s], PRE_PE.total)
                        pe.sem_inc(cell_pe[s], CELL_PE.total)
                        pe.sem_inc(post_pe[s], POST_PE.total)

                    def per_graph(dst, stationary, moving, transpose=False):
                        for b in range(GB):
                            if transpose:
                                last = pe.transpose(dst[:, b, :], stationary[:, b, :], ident[:])
                            else:
                                last = pe.matmul(dst[:, b, :], stationary[:, b, :], moving, start=True, stop=True)
                        return last

                    def pre(it, s):
                        def before(step):
                            sems, steps = (pre_dve, PRE_DVE) if step in PRE_DVE.at else (pre_act, PRE_ACT)
                            if s:
                                pe.wait_ge(sems[0], steps.done(it, step))
                            else:
                                pe.wait_ge(sems[1], steps.done_before(it, step))
                        before("xw1")
                        pe.wait_ge(x_in[s], it * 32 + 32)
                        for b in range(GB):
                            last = pe.matmul(PB[0][:, 3 * b:3 * b + 3], x_f[s][:, b, :], gate_w[:], start=True, stop=True)
                        last.then_inc(pre_pe[s], 1)
                        before("h2")
                        pe.matmul(PB[1][:], w_inT[:], flat(x_t[s][:]), start=True, stop=True).then_inc(pre_pe[s], 1)
                        pe.wait_ge(pre_dve[s], PRE_DVE.done(it, "gates"))
                        pe.matmul(PB[0][:], w_outT[:], flat(x_t[s][:]), start=True, stop=True).then_inc(pre_pe[s], 1)
                        pe.wait_ge(pre_dve[s], PRE_DVE.done(it, "x1"))
                        per_graph(PT[1], x1[s], None, True).then_inc(pre_pe[s], 1)
                        pe.wait_ge(pre_act[s], PRE_ACT.done(it, "x1t"))
                        per_graph(PT[0], x1T, wg0[:]).then_inc(pre_pe[s], 1)
                        pe.wait_ge(pre_dve[s], PRE_DVE.done(it, "xw0"))
                        per_graph(PT[1], xw, adjT[:]).then_inc(pre_pe[s], 1)
                        pe.wait_ge(pre_act[s], PRE_ACT.done(it, "h1"))
                        per_graph(PT[0], h1T, wg1[:]).then_inc(pre_pe[s], 1)
                        pe.wait_ge(pre_dve[s], PRE_DVE.done(it, "xw1"))
                        per_graph(PT[1], xw, adjT[:]).then_inc(pre_pe[s], 1)

                    def cell(it, s, u):
                        p, j, nw, b0, nb = UNITS[u]
                        n = nw * nb
                        src = hT[s] if p == 1 else seq[s]
                        xs = src[:, b0:b0 + nb, bass.ds(j, nw, p)] if p > 1 else src[:, b0:b0 + nb, :]
                        slot = {GI: GATE[s][0][:, 0:n], GG: GATE[s][0][:, 256:256 + n],
                                GF: GATE[s][1][:, 0:n], GO: GATE[s][1][:, 256:256 + n]}

                        def out3(g):
                            return slot[g].rearrange("p (b w) -> p b w", b=nb)

                        def wx(g):
                            return wihT[:, p - 1, g * 128:(g + 1) * 128]

                        def wh(g):
                            return whhT[:, p - 1, g * 128:(g + 1) * 128]

                        if u == 0:
                            pe.wait_ge(pre_act[s], PRE_ACT.done(it, "h2"))
                            pe.wait_ge(cell_dve[s], CELL_DVE.done_before(it, f"{NU - 1}h"))
                        elif j == 0:
                            pe.wait_ge(cell_dve[s], CELL_DVE.done(it, f"{u - 1}h"))
                        else:
                            pe.wait_ge(cell_act[s], CELL_ACT.done(it, f"{u - 1}o"))
                        if j == 0:
                            pe.matmul(out3(GI), wx(GI), xs, start=True, stop=True)
                            pe.matmul(out3(GG), wx(GG), xs, start=True, stop=True).then_inc(cell_pe[s], 1)
                            pe.matmul(out3(GO), wx(GO), xs, start=True, stop=True).then_inc(cell_pe[s], 1)
                            return
                        hs = hid[s][:, 0:n]
                        for k, g in enumerate((GI, GG, GF, GO)):
                            pe.matmul(out3(g), wx(g), xs, start=(k % 2 == 0), stop=False, skip_group_check=True)
                        pe.wait_ge(cell_dve[s], CELL_DVE.done(it, f"{u - 1}h"))
                        for k, g in enumerate((GI, GG, GF, GO)):
                            last = pe.matmul(slot[g], wh(g), hs, start=False, stop=True, skip_group_check=True)
                            if k % 2:
                                last.then_inc(cell_pe[s], 1)

                    def post(it, s):
                        prev, before = 1 - s, (POST_DVE.done if s else POST_DVE.done_before)
                        pe.wait_ge(cell_dve[s], CELL_DVE.done(it, f"{NU - 1}h"))
                        pe.wait_ge(post_dve[prev], before(it, "bnb"))
                        per_graph(QT[0], seq[s], None, True).then_inc(post_pe[s], 1)
                        pe.wait_ge(post_dve[s], POST_DVE.done(it, "x2"))
                        per_graph(QT[1], x2[s], a_hatT[:]).then_inc(post_pe[s], 1)
                        pe.wait_ge(post_act[s], POST_ACT.done(it, "agg"))
                        for h in range(H1):
                            pe.matmul(QB[h][:], w1T[:, h * 128:(h + 1) * 128], flat(agg[s][:]), start=True,
                                      stop=True).then_inc(post_pe[s], 1)

                    with pe.Fori(0, NIT) as it:
                        for s in range(S):
                            pre(it, s)
                        for u in range(NU):
                            for s in range(S):
                                cell(it, s, u)
                        for s in range(S):
                            post(it, s)

                @block.scalar
                def _(act):
                    for s in range(S):
                        act.sem_inc(pre_act[s], PRE_ACT.total)
                        act.sem_inc(cell_act[s], CELL_ACT.total)
                        act.sem_inc(post_act[s], POST_ACT.total)

                    def pre(it, s):
                        act.wait_ge(pre_dve[s], PRE_DVE.done(it, "gates"))
                        act.activation(sg[s][:], gz[s][:], ACT.Sigmoid).then_inc(pre_act[s], 1)
                        act.wait_ge(pre_pe[s], PRE_PE.done(it, "x1t"))
                        act.activation(x1T[:], PT[1], ACT.Copy).then_inc(pre_act[s], 1)
                        act.wait_ge(pre_pe[s], PRE_PE.done(it, "ax0"))
                        act.activation(h1T[:], PT[1], ACT.Relu).then_inc(pre_act[s], 1)
                        act.wait_ge(pre_pe[s], PRE_PE.done(it, "ax1"))
                        act.activation(hT[s][:], PT[1], ACT.Relu).then_inc(pre_act[s], 1)

                    def cell(it, s, u):
                        p, j, nw, b0, nb = UNITS[u]
                        n = nw * nb

                        def gate(dst, g, func):
                            k, at = {GI: (0, 0), GG: (0, 256), GF: (1, 0), GO: (1, 256)}[g]
                            col = 4 * (p - 1) + g
                            act.activation(dst[s][:, 0:n], GATE[s][k][:, at:at + n], func,
                                           bias=b_cell[:, col:col + 1]).then_inc(cell_act[s], 1)

                        act.wait_ge(cell_pe[s], CELL_PE.done(it, f"{u}ig"))
                        gate(gi, GI, ACT.Sigmoid)
                        gate(gg, GG, ACT.Tanh)
                        act.wait_ge(cell_pe[s], CELL_PE.done(it, f"{u}fo"))
                        if j:
                            gate(gf, GF, ACT.Sigmoid)
                        gate(go, GO, ACT.Sigmoid)
                        act.wait_ge(cell_dve[s], CELL_DVE.done(it, f"{u}c"))
                        act.activation(ct[s][:, 0:n], cc[s][:, 0:n], ACT.Tanh).then_inc(cell_act[s], 1)

                    def post(it, s):
                        act.wait_ge(agg_out[s], it * 16 + 16)
                        act.wait_ge(post_pe[s], POST_PE.done(it, "agg"))
                        act.activation(agg[s][:], QT[1], ACT.Copy).then_inc(post_act[s], 1)

                    with act.Fori(0, NIT) as it:
                        for s in range(S):
                            pre(it, s)
                        for u in range(NU):
                            for s in range(S):
                                cell(it, s, u)
                        for s in range(S):
                            post(it, s)

                @block.vector
                def _(dve):
                    for s in range(S):
                        dve.sem_inc(pre_dve[s], PRE_DVE.total)
                        dve.sem_inc(cell_dve[s], CELL_DVE.total)
                        dve.sem_inc(post_dve[s], POST_DVE.total)

                    def pre(it, s):
                        def own(step):
                            dve.wait_ge(pre_dve[s], PRE_DVE.done(it, step))

                        def wide(m):
                            return m[:].unsqueeze(1).broadcast_to([128, GB, m.shape[-1]])

                        dve.wait_ge(pre_pe[s], PRE_PE.done(it, "gates"))
                        dve.tensor_tensor(gz[s][:], PB[0][:, 0:3 * GB].rearrange("p (b g) -> p b g", g=3), wide(gate_b),
                                          ALU.add).then_inc(pre_dve[s], 1)
                        dve.wait_ge(pre_pe[s], PRE_PE.done(it, "in"))
                        dve.tensor_tensor(u_in[:], PT[1], wide(eb), ALU.add).then_inc(pre_dve[s], 1)
                        dve.wait_ge(pre_pe[s], PRE_PE.done(it, "out"))
                        dve.tensor_tensor(u_out[:], PT[0], wide(oeb), ALU.add).then_inc(pre_dve[s], 1)
                        dve.wait_ge(pre_act[s], PRE_ACT.done(it, "gates"))
                        settle(dve)
                        for b in range(GB):
                            last = dve.tensor_scalar(y1[s][:, b, :], x_t[s][:, b, :], sg[s][:, b, 2:3], None, ALU.mult)
                        last.then_inc(pre_dve[s], 1)
                        for k, (u, name) in enumerate(((u_in, "loop"), (u_out, "acc_in"))):
                            own(name)
                            for b in range(GB):
                                last = dve.scalar_tensor_tensor(y1[s][:, b, :], u[:, b, :], sg[s][:, b, k:k + 1],
                                                                y1[s][:, b, :], ALU.mult, ALU.add)
                            last.then_inc(pre_dve[s], 1)
                        own("acc_out")
                        dve.scalar_tensor_tensor(y1[s][:], y1[s][:], 0.0, x_t[s][:], ALU.max, ALU.add).then_inc(pre_dve[s], 1)
                        own("y")
                        settle(dve)
                        for b in range(GB):
                            last = dve.bn_stats(ln_s[s][:, b, :], y1[s][:, b, :])
                        last.then_inc(pre_dve[s], 1)
                        own("stats")
                        settle(dve)
                        for b in range(GB):
                            last = dve.bn_aggr(ln_mv[s][:, b, :], ln_s[s][:, b, :])
                        last.then_inc(pre_dve[s], 1)
                        dve.wait_ge(pre_pool[s], PRE_POOL.done(it, "rstd"))
                        settle(dve)
                        for b in range(GB):
                            last = dve.tensor_scalar(x1[s][:, b, :], y1[s][:, b, :], ln_mv[s][:, b, 0:1],
                                                     ln_r[s][:, b:b + 1], ALU.subtract, ALU.mult)
                        last.then_inc(pre_dve[s], 1)
                        dve.wait_ge(pre_pe[s], PRE_PE.done(it, "xw0"))
                        dve.tensor_tensor(xw[:], PT[0], wide(bg0), ALU.add).then_inc(pre_dve[s], 1)
                        dve.wait_ge(pre_pe[s], PRE_PE.done(it, "xw1"))
                        dve.tensor_tensor(xw[:], PT[0], wide(bg1), ALU.add).then_inc(pre_dve[s], 1)

                    def cell(it, s, u):
                        p, j, nw, b0, nb = UNITS[u]
                        n = nw * nb
                        a, b, c, d = (x[s][:, 0:n] for x in (gi, gg, cc, ig))
                        dve.wait_ge(cell_act[s], CELL_ACT.done(it, f"{u}g"))
                        dve.tensor_tensor(c if j == 0 else d, a, b, ALU.mult).then_inc(cell_dve[s], 1)
                        if j:
                            dve.wait_ge(cell_act[s], CELL_ACT.done(it, f"{u}f"))
                            dve.tensor_tensor(c, gf[s][:, 0:n], c, ALU.mult).then_inc(cell_dve[s], 1)
                            dve.wait_ge(cell_dve[s], CELL_DVE.done(it, f"{u}fc"))
                            dve.tensor_tensor(c, c, d, ALU.add).then_inc(cell_dve[s], 1)
                        dve.wait_ge(cell_act[s], CELL_ACT.done(it, f"{u}t"))
                        if j == p - 1:
                            o = seq[s][:, b0:b0 + nb, bass.ds(j, nw, p)] if p > 1 else seq[s][:, b0:b0 + nb, :]
                        else:
                            o = hid[s][:, 0:n].rearrange("p (b w) -> p b w", b=nb)
                        dve.tensor_tensor(o, go[s][:, 0:n].rearrange("p (b w) -> p b w", b=nb),
                                          ct[s][:, 0:n].rearrange("p (b w) -> p b w", b=nb), ALU.mult).then_inc(cell_dve[s], 1)

                    def post(it, s):
                        def own(step):
                            dve.wait_ge(post_dve[s], POST_DVE.done(it, step))
                            settle(dve)

                        dve.wait_ge(post_pe[s], POST_PE.done(it, "hT"))
                        dve.tensor_tensor(y2[s][:], QT[0], x1[s][:], ALU.add).then_inc(post_dve[s], 1)
                        own("y")
                        for b in range(GB):
                            last = dve.bn_stats(post_s[s][:, b, :], y2[s][:, b, :])
                        last.then_inc(post_dve[s], 1)
                        own("stats")
                        for b in range(GB):
                            last = dve.bn_aggr(post_mv[s][:, b, :], post_s[s][:, b, :])
                        last.then_inc(post_dve[s], 1)
                        dve.wait_ge(x2_out[s], it * 16 + 16)
                        dve.wait_ge(post_pool[s], POST_POOL.done(it, "rstd"))
                        settle(dve)
                        for b in range(GB):
                            last = dve.tensor_scalar(x2[s][:, b, :], y2[s][:, b, :], post_mv[s][:, b, 0:1],
                                                     post_r[s][:, b:b + 1], ALU.subtract, ALU.mult)
                        last.then_inc(post_dve[s], 1)
                        for h, name in enumerate(("w1a", "w1b")):
                            dve.wait_ge(post_pe[s], POST_PE.done(it, name))
                            settle(dve)
                            dve.bn_stats(bn1_stats[:, h, bass.ds(it * S + s, 1), :].rearrange("p a b -> p (a b)"),
                                         QB[h][:]).then_inc(post_dve[s], 1)

                    with dve.Fori(0, NIT) as it:
                        for s in range(S):
                            pre(it, s)
                        for u in range(NU):
                            for s in range(S):
                                cell(it, s, u)
                        for s in range(S):
                            post(it, s)

                @block.gpsimd
                def _(pool):
                    for s in range(S):
                        pool.sem_inc(pre_pool[s], PRE_POOL.total)
                        pool.sem_inc(post_pool[s], POST_POOL.total)

                    def rstd(r, mv, done, steps, it):
                        settle(pool)
                        pool.tensor_scalar(r[:], mv[:, :, 1], EPS, None, ALU.add).then_inc(done, 1)
                        pool.wait_ge(done, steps.done(it, "veps"))
                        pool.tensor_tensor(r[:], r[:], minus_half[:], ALU.pow).then_inc(done, 1)

                    with pool.Fori(0, NIT) as it:
                        for s in range(S):
                            pool.wait_ge(pre_dve[s], PRE_DVE.done(it, "aggr"))
                            rstd(ln_r[s], ln_mv[s], pre_pool[s], PRE_POOL, it)
                        for s in range(S):
                            pool.wait_ge(post_dve[s], POST_DVE.done(it, "aggr"))
                            rstd(post_r[s], post_mv[s], post_pool[s], POST_POOL, it)

        bn1_mv = sb("bn1_mv", [128, H1, 2])
        bn1_scale, bn1_shift = sb("bn1_scale", [128, H1]), sb("bn1_shift", [128, H1])
        bn2_mv = sb("bn2_mv", [128, 2])
        bn2_scale, bn2_shift = sb("bn2_scale", [128, 1]), sb("bn2_shift", [128, 1])
        bn_tmp = sb("bn_tmp", [128, 2 * H1])

        def bn_dve(dve, s_dve, s_pool, n, stats, mv, b, g, be, scale, shift):
            count = [0]

            def step(ins):
                ins.then_inc(s_dve, 1)
                count[0] += 1
                dve.wait_ge(s_dve, count[0])
            for k in range(n):
                step(dve.bn_aggr(mv[k], stats[k]))
            mean_ap = bn_mean(mv, n)
            step(dve.tensor_tensor(bn_tmp[:, 0:n], mean_ap, b, ALU.add))
            step(dve.tensor_tensor(bn_tmp[:, n:2 * n], b, bn_tmp[:, 0:n], ALU.subtract))
            dve.wait_ge(s_pool, 2)
            step(dve.tensor_tensor(scale, scale, g, ALU.mult))
            step(dve.tensor_tensor(bn_tmp[:, 0:n], bn_tmp[:, n:2 * n], scale, ALU.mult))
            step(dve.tensor_tensor(shift, bn_tmp[:, 0:n], be, ALU.add))
            return count[0]

        def bn_mean(mv, n):
            return bn1_mv[:, :, 0] if n == H1 else bn2_mv[:, 0:1]

        def bn_pool(pool, s_dve, s_pool, n, var, scale):
            pool.wait_ge(s_dve, n)
            pool.tensor_scalar(scale, var, EPS, None, ALU.add).then_inc(s_pool, 1)
            pool.wait_ge(s_pool, 1)
            pool.tensor_tensor(scale, scale, minus_half[:, 0:n], ALU.pow).then_inc(s_pool, 1)

        with ExitStack() as two:
            bn1_dve, bn1_pool = sem("bn1_dve", two), sem("bn1_pool", two)
            mlp_pe, mlp_act, mlp_dve = ([sem(f"{n}{s}", two) for s in range(S)] for n in ("mlp_pe", "mlp_act", "mlp_dve"))
            hid1 = [sb(f"hid1_{s}", [128, H1, C], two) for s in range(S)]
            BN1_DONE = H1 + 5
            W1B = [[bank[0], bank[1]], [bank[2], bank[3]]]
            W2B = [bank[4], bank[5]]

            with nc.Block() as block:
                def cols(it, s):
                    return agg_all[:, bass.ds(it * (S * GB) + s * GB, GB), :]

                @block.gpsimd
                def _(pool):
                    bn_pool(pool, bn1_dve, bn1_pool, H1, bn1_mv[:, :, 1], bn1_scale[:])

                @block.tensor
                def _(pe):
                    for s in range(S):
                        pe.sem_inc(mlp_pe[s], MLP_PE.total)

                    with pe.Fori(0, NIT) as it:
                        for s in range(S):
                            for h in range(H1):
                                pe.wait_ge(mlp_act[s], MLP_ACT.done_before(it, f"h{h}"))
                                settle(pe)
                                pe.matmul(W1B[s][h][:], w1T[:, h * 128:(h + 1) * 128], cols(it, s), start=True,
                                          stop=True).then_inc(mlp_pe[s], 1)
                        for s in range(S):
                            pe.wait_ge(mlp_act[s], MLP_ACT.done_before(it, "out"))
                            pe.wait_ge(mlp_dve[s], MLP_DVE.done_before(it, "bn"))
                            for h in range(H1):
                                pe.wait_ge(mlp_act[s], MLP_ACT.done(it, f"h{h}"))
                                last = pe.matmul(W2B[s][:], w2T[:, h, :], hid1[s][:, h, :], start=(h == 0),
                                                 stop=(h == H1 - 1))
                            last.then_inc(mlp_pe[s], 1)

                @block.scalar
                def _(act):
                    for s in range(S):
                        act.sem_inc(mlp_act[s], MLP_ACT.total)
                    act.wait_ge(bn1_dve, BN1_DONE)
                    with act.Fori(0, NIT) as it:
                        for s in range(S):
                            for h, name in enumerate(("w1a", "w1b")):
                                act.wait_ge(mlp_pe[s], MLP_PE.done(it, name))
                                act.activation(hid1[s][:, h, :], W1B[s][h][:], ACT.Relu, bias=bn1_shift[:, h:h + 1],
                                               scale=bn1_scale[:, h:h + 1]).then_inc(mlp_act[s], 1)
                        for s in range(S):
                            act.wait_ge(mlp_dve[s], MLP_DVE.done(it, "bn"))
                            settle(act)
                            act.activation(cols(it, s), W2B[s][:].rearrange("p (b n) -> p b n", b=GB),
                                           ACT.Copy).then_inc(mlp_act[s], 1)

                @block.vector
                def _(dve):
                    for s in range(S):
                        dve.sem_inc(mlp_dve[s], MLP_DVE.total)
                    n = bn_dve(dve, bn1_dve, bn1_pool, H1, [bn1_stats[:, h, :, :].rearrange("p a b -> p (a b)") for h in range(H1)],
                               [bn1_mv[:, h, :] for h in range(H1)], bn1_par[:, 0, :], bn1_par[:, 1, :], bn1_par[:, 2, :],
                               bn1_scale[:], bn1_shift[:])
                    assert n == BN1_DONE
                    with dve.Fori(0, NIT) as it:
                        for s in range(S):
                            dve.wait_ge(mlp_pe[s], MLP_PE.done(it, "w2"))
                            settle(dve)
                            dve.bn_stats(bn2_stats[:, bass.ds(it * S + s, 1), :].rearrange("p a b -> p (a b)"),
                                         W2B[s][:]).then_inc(mlp_dve[s], 1)

        with ExitStack() as three:
            def sb3(name, shape):
                return sb(name, shape, three)

            bn2_dve, bn2_pool = sem("bn2_dve", three), sem("bn2_pool", three)
            ones_set = sem("ones_set", three)
            x2_in = [sem(f"x2_in{s}", three) for s in range(S)]
            out_done = [sem(f"out_done{s}", three) for s in range(S)]
            att_pe, att_act, att_dve, att_pool = ([sem(f"{n}{s}", three) for s in range(S)]
                                                  for n in ("att_pe", "att_act", "att_dve", "att_pool"))
            x2b = [sb3(f"x2b{s}", [128, GB, D]) for s in range(S)]
            z, y3, x3, x3T, qT, kT, fin = ([sb3(f"{n}{s}", [128, GB, D]) for s in range(S)]
                                           for n in ("z", "y3_", "x3_", "x3T", "qT", "kT", "fin"))
            v = [sb3(f"v{s}", [128, GB, NH, HD + 1]) for s in range(S)]
            pr = [[sb3(f"pr{s}{h}", [128, GB, N]) for h in range(NH)] for s in range(S)]
            prT = [[sb3(f"prT{s}{k}", [128, GB, N]) for k in range(2)] for s in range(S)]
            mx = [sb3(f"mx{s}", [128, NH, GB]) for s in range(S)]
            rec = [sb3(f"rec{s}", [128, GB, NH]) for s in range(S)]
            a_s, a_mv, a_r = [sb3(f"a_s{s}", [128, GB, 6]) for s in range(S)], [sb3(f"a_mv{s}", [128, GB, 2]) for s in range(S)], [sb3(f"a_r{s}", [128, GB]) for s in range(S)]
            GT, GK = [tile[0], tile[1]], [bank[0], bank[1]]
            ST = [tile[2], tile[3]]
            PTB = [tile[4], tile[5]]
            OB = [bank[6][:, 0:2 * NH * (HD + 1)].rearrange("p (b h e) -> p b h e", b=2, h=NH),
                  bank[7][:, 0:2 * NH * (HD + 1)].rearrange("p (b h e) -> p b h e", b=2, h=NH)]
            BN2_DONE = 1 + 5
            SCALE = float(1.0 / HD ** 0.5)

            def group3(it, s):
                return bass.ds(it * (S * GB) + s * GB, GB)

            def stage(steps, sems, s, it, name):
                return (sems[0], steps.done(it, name)) if s else (sems[1], steps.done_before(it, name))

            with nc.Block() as block:
                @block.sync
                def _(sp):
                    for s in range(S):
                        sp.sem_inc(out_done[s], 16)
                    with sp.Fori(0, NIT) as it:
                        for s in range(S):
                            sp.wait_ge(att_dve[s], ATT_DVE.done_before(it, "y"))
                            settle(sp)
                            sp.dma_start(x2b[s][:], x2_dram[:, group3(it, s), :]).then_inc(x2_in[s], 16)
                        for s in range(S):
                            sp.wait_ge(att_dve[s], ATT_DVE.done(it, "out"))
                            settle(sp)
                            sp.dma_start(out[:, group3(it, s), :], fin[s][:]).then_inc(out_done[s], 16)
                    for s in range(S):
                        sp.wait_ge(out_done[s], 16 * NIT + 16)

                @block.gpsimd
                def _(pool):
                    for s in range(S):
                        pool.sem_inc(att_pool[s], ATT_POOL.total)
                        pool.memset(v[s][:, :, :, HD:HD + 1], 1.0).then_inc(ones_set, 1)
                    bn_pool(pool, bn2_dve, bn2_pool, 1, bn2_mv[:, 1:2], bn2_scale[:])

                    def rstd(it, s, tag):
                        pool.wait_ge(att_dve[s], ATT_DVE.done(it, "aggr" + tag))
                        settle(pool)
                        pool.tensor_scalar(a_r[s][:], a_mv[s][:, :, 1], EPS, None, ALU.add).then_inc(att_pool[s], 1)
                        pool.wait_ge(att_pool[s], ATT_POOL.done(it, "veps" + tag))
                        pool.tensor_tensor(a_r[s][:], a_r[s][:], minus_half[:], ALU.pow).then_inc(att_pool[s], 1)

                    with pool.Fori(0, NIT) as it:
                        for s in range(S):
                            rstd(it, s, "")
                            for h in range(NH):
                                pool.wait_ge(att_dve[s], ATT_DVE.done(it, f"max{h}"))
                                pool.tensor_tensor(pr[s][h][:], pr[s][h][:],
                                                   mx[s][:, h, :].unsqueeze(2).broadcast_to([128, GB, N]),
                                                   ALU.subtract).then_inc(att_pool[s], 1)
                            rstd(it, s, "3")

                @block.tensor
                def _(pe):
                    for s in range(S):
                        pe.sem_inc(att_pe[s], ATT_PE.total)

                    def att(it, s):
                        def before(steps, sems, name):
                            pe.wait_ge(*stage(steps, sems, s, it, name))

                        def act_done(name):
                            pe.wait_ge(att_act[s], ATT_ACT.done(it, name))

                        def dve_done(name):
                            pe.wait_ge(att_dve[s], ATT_DVE.done(it, name))

                        def per_graph(dst, src):
                            for b in range(GB):
                                last = pe.transpose(dst[:, b, :], src[:, b, :], ident[:])
                            last.then_inc(att_pe[s], 1)

                        before(ATT_ACT, att_act, "v")
                        act_done("z")
                        per_graph(GT[0], z[s])
                        before(ATT_DVE, att_dve, "k")
                        dve_done("x3")
                        per_graph(GT[1], x3[s])
                        act_done("x3t")
                        pe.matmul(GK[0][:], w3[:, 0:D], flat(x3T[s][:]), start=True, stop=True).then_inc(att_pe[s], 1)
                        pe.matmul(GK[1][:], w3[:, D:2 * D], flat(x3T[s][:]), start=True, stop=True).then_inc(att_pe[s], 1)
                        act_done("q")
                        for b in range(GB):
                            last = pe.matmul(GT[0][:, b, :], x3T[s][:, b, :], w3[:, 2 * D:3 * D], start=True, stop=True)
                        last.then_inc(att_pe[s], 1)

                        def scores(h):
                            if h == 0:
                                before(ATT_DVE, att_dve, "m2")
                                dve_done("k")
                            elif h == 1:
                                before(ATT_DVE, att_dve, "m3")
                            else:
                                dve_done(f"m{h - 2}")
                            for b in range(GB):
                                last = pe.matmul(ST[h % 2][:, b, :], qT[s][h * HD:(h + 1) * HD, b, :],
                                                 kT[s][h * HD:(h + 1) * HD, b, :], start=True, stop=True)
                            last.then_inc(att_pe[s], 1)

                        def turn(h):
                            if h < 2:
                                before(ATT_ACT, att_act, f"pt{h + 2}")
                            act_done(f"exp{h}")
                            per_graph(PTB[h % 2], pr[s][h])

                        def values(h):
                            if h == 0:
                                before(ATT_DVE, att_dve, "att")
                            act_done(f"pt{h}")
                            for b in range(GB):
                                last = pe.matmul(OB[b // 2][:, b % 2, h, :], prT[s][h % 2][:, b, :], v[s][:, b, h, :],
                                                 start=True, stop=True)
                            last.then_inc(att_pe[s], 1)

                        scores(0)
                        scores(1)
                        turn(0)
                        scores(2)
                        turn(1)
                        scores(3)
                        values(0)
                        turn(2)
                        values(1)
                        turn(3)
                        values(2)
                        values(3)

                    pe.wait_ge(ones_set, S)
                    with pe.Fori(0, NIT) as it:
                        for s in range(S):
                            att(it, s)

                @block.scalar
                def _(act):
                    for s in range(S):
                        act.sem_inc(att_act[s], ATT_ACT.total)
                    act.wait_ge(bn2_dve, BN2_DONE)

                    def att(it, s):
                        def pe_done(name):
                            act.wait_ge(att_pe[s], ATT_PE.done(it, name))

                        act.wait_ge(att_pe[s], ATT_PE.done_before(it, "zt"))
                        settle(act)
                        act.activation(z[s][:], agg_all[:, group3(it, s), :], ACT.Identity, bias=bn2_shift[:, 0:1],
                                       scale=bn2_scale[:, 0:1]).then_inc(att_act[s], 1)
                        pe_done("x3t")
                        act.activation(x3T[s][:], GT[1], ACT.Copy).then_inc(att_act[s], 1)
                        pe_done("q")
                        act.activation(qT[s][:], GT[0], ACT.Copy).then_inc(att_act[s], 1)
                        pe_done("v")
                        act.activation(v[s][:, :, :, 0:HD], GT[0].rearrange("p b (h e) -> p b h e", h=NH),
                                       ACT.Copy).then_inc(att_act[s], 1)

                        def exp(h):
                            act.wait_ge(att_pool[s], ATT_POOL.done(it, f"sub{h}"))
                            act.activation(pr[s][h][:], pr[s][h][:], ACT.Exp).then_inc(att_act[s], 1)

                        def turned(h):
                            pe_done(f"pt{h}")
                            if h >= 2:
                                pe_done(f"pv{h - 2}")
                            act.activation(prT[s][h % 2][:], PTB[h % 2], ACT.Copy).then_inc(att_act[s], 1)

                        exp(0)
                        exp(1)
                        turned(0)
                        exp(2)
                        turned(1)
                        exp(3)
                        turned(2)
                        turned(3)

                    with act.Fori(0, NIT) as it:
                        for s in range(S):
                            att(it, s)

                @block.vector
                def _(dve):
                    for s in range(S):
                        dve.sem_inc(att_dve[s], ATT_DVE.total)
                    n = bn_dve(dve, bn2_dve, bn2_pool, 1, [bn2_stats[:].rearrange("p a b -> p (a b)")], [bn2_mv[:]],
                               bn2_par[:, 0:1], bn2_par[:, 1:2], bn2_par[:, 2:3], bn2_scale[:], bn2_shift[:])
                    assert n == BN2_DONE

                    def att(it, s):
                        def pe_done(name):
                            dve.wait_ge(att_pe[s], ATT_PE.done(it, name))

                        def own(name):
                            dve.wait_ge(att_dve[s], ATT_DVE.done(it, name))

                        def norm(dst, src, first, tag, last_step):
                            own(first)
                            settle(dve)
                            for b in range(GB):
                                last = dve.bn_stats(a_s[s][:, b, :], src[:, b, :])
                            last.then_inc(att_dve[s], 1)
                            own("stats" + tag)
                            settle(dve)
                            for b in range(GB):
                                last = dve.bn_aggr(a_mv[s][:, b, :], a_s[s][:, b, :])
                            last.then_inc(att_dve[s], 1)
                            dve.wait_ge(att_pool[s], ATT_POOL.done(it, "rstd" + tag))
                            settle(dve)
                            for b in range(GB):
                                last = dve.tensor_scalar(dst[:, b, :], src[:, b, :], a_mv[s][:, b, 0:1],
                                                         a_r[s][:, b:b + 1], ALU.subtract, ALU.mult)
                            last.then_inc(att_dve[s], 1)

                        dve.wait_ge(x2_in[s], it * 16 + 16)
                        pe_done("zt")
                        dve.tensor_tensor(y3[s][:], GT[0], x2b[s][:], ALU.add).then_inc(att_dve[s], 1)
                        norm(x3[s], y3[s], "y", "", "x3")
                        pe_done("k")
                        dve.tensor_copy(kT[s][:], GT[1]).then_inc(att_dve[s], 1)
                        for h in range(NH):
                            pe_done(f"sc{h}")
                            dve.scalar_tensor_tensor(pr[s][h][:], ST[h % 2], SCALE,
                                                     mask[:].unsqueeze(1).broadcast_to([128, GB, N]),
                                                     ALU.mult, ALU.add).then_inc(att_dve[s], 1)
                            own(f"m{h}")
                            dve.reduce_max(mx[s][:, h, :], pr[s][h][:], AX).then_inc(att_dve[s], 1)
                        pe_done("pv3")
                        settle(dve)
                        for k in range(2):
                            last = dve.reciprocal(rec[s][:, 2 * k:2 * k + 2, :], OB[k][:, :, :, HD])
                        last.then_inc(att_dve[s], 1)
                        own("rec")
                        for k in range(2):
                            last = dve.tensor_tensor(
                                y3[s][:, 2 * k:2 * k + 2, :].rearrange("p b (h e) -> p b h e", h=NH), OB[k][:, :, :, 0:HD],
                                rec[s][:, 2 * k:2 * k + 2, :].unsqueeze(3).broadcast_to([128, 2, NH, HD]), ALU.mult)
                        last.then_inc(att_dve[s], 1)
                        own("att")
                        dve.tensor_tensor(y3[s][:], y3[s][:], x3[s][:], ALU.add).then_inc(att_dve[s], 1)
                        dve.wait_ge(out_done[s], it * 16 + 16)
                        norm(fin[s], y3[s], "y3", "3", "out")

                    with dve.Fori(0, NIT) as it:
                        for s in range(S):
                            att(it, s)


def kernel(**inputs):
    import numpy as np
    import concourse.bacc as _bacc
    from concourse.bass_utils import run_bass_kernel_spmd as _run

    a = {k: np.asarray(v) for k, v in inputs.items()}
    l0, l1, l2 = "L0_gnn_", "L1_gnn_", "L2_gnn_"

    def gates_last(b):
        return b.reshape(MAXW, 4, 128).transpose(2, 0, 1).reshape(128, MAXW * 4)

    lay = {
        "x_t": a["x"].transpose(1, 0, 2), "x_f": a["x"].transpose(2, 0, 1),
        "adj": a["adj"], "adjT": a["adj"].T,
        "eb": a[l0 + "edge_bias"], "oeb": a[l0 + "out_edge_bias"],
        "gate_w": np.concatenate([a[l0 + "gate_weight"], a[l0 + "out_gate_weight"], a[l0 + "loop_gate"]], 1),
        "gate_b": np.concatenate([a[l0 + "bias_gate"], a[l0 + "out_bias_gate"]], 1),
        "wg0": a[l1 + "Wg0"], "wg1": a[l1 + "Wg1"], "bg0": a[l1 + "bg0"], "bg1": a[l1 + "bg1"],
        "wihT": a[l1 + "Wih"].transpose(2, 0, 1), "whhT": a[l1 + "Whh"].transpose(2, 0, 1),
        "bih": gates_last(a[l1 + "bih"]), "bhh": gates_last(a[l1 + "bhh"]),
        "w1T": a[l2 + "W1"].T, "w2T": a[l2 + "W2"].T.reshape(H1, 128, D).transpose(1, 0, 2),
        "bn1": np.stack([a[l2 + n].reshape(H1, 128).T for n in ("b1", "g1", "be1")], 1),
        "bn2": np.stack([a[l2 + n] for n in ("b2", "g2", "be2")], 1),
        "w3": a["L3_gnn_W"],
    }
    nc = _bacc.Bacc("TRN2", target_bir_lowering=False, num_devices=1)
    arrays = {f"in_{k}": np.ascontiguousarray(v) for k, v in lay.items()}
    t = {k: nc.dram_tensor(f"in_{k}", arrays[f"in_{k}"].shape, F32, kind="ExternalInput").ap() for k in lay}
    out = nc.dram_tensor("out_dram", (N, B, D), F32, kind="ExternalOutput").ap()
    build(nc, t, out)
    r = _run(nc, [arrays], core_ids=[0])
    return np.ascontiguousarray(r.results[0]["out_dram"].transpose(1, 0, 2))
```

```python
from contextlib import ExitStack

import concourse.bass as bass
from concourse import mybir

F32 = mybir.dt.float32
ALU = mybir.AluOpType
ACT = mybir.ActivationFunctionType
AX = mybir.AxisListType.X

B, N, D = 128, 128, 128
GB = 4
S = 2
NIT = B // (GB * S)
NG = B // GB
C = GB * N
H1 = 2
NH, HD = 4, 32
EPS = 1e-5
MASKED = -3.0e38
MAXW = 4
GI, GF, GG, GO = range(4)


class Steps:

    def __init__(self, *names):
        self.at = {n: k + 1 for k, n in enumerate(names)}
        self.total = len(names)

    def done(self, it, name):
        return it * self.total + (self.total + self.at[name])

    def done_before(self, it, name):
        return it * self.total + self.at[name]


UNITS = [(1, 0, N, 0, GB // 2), (1, 0, N, GB // 2, GB // 2)]
UNITS += [(p, j, N // p, 0, GB) for p in range(2, MAXW + 1) for j in range(p)]
NU = len(UNITS)

PRE_PE = Steps("gates", "in", "out", "x1t", "xw0", "ax0", "xw1", "ax1")
PRE_DVE = Steps("gates", "in", "acc_in", "out", "acc_out", "y", "stats", "aggr", "x1", "xw0", "xw1")
PRE_ACT = Steps("gates", "loop", "x1t", "h1", "h2")
PRE_POOL = Steps("veps", "rstd")
CELL_PE = Steps(*[f"{u}{x}" for u in range(NU) for x in ("ig", "fo")])
CELL_ACT = Steps(*[f"{u}{x}" for u in range(NU) for x in (("i", "g", "o", "t") if UNITS[u][1] == 0 else ("i", "g", "f", "o", "t"))])
CELL_DVE = Steps(*[f"{u}{x}" for u in range(NU) for x in (("c", "h") if UNITS[u][1] == 0 else ("ig", "fc", "c", "h"))])
POST_PE = Steps("hT", "agg", "w1a", "w1b")
POST_DVE = Steps("y", "stats", "aggr", "x2", "bna", "bnb")
POST_ACT = Steps("agg")
POST_POOL = Steps("veps", "rstd")

KEEP = Steps("keep")

MLP_PE = Steps("w1a", "w1b", "w2")
MLP_ACT = Steps("h0", "h1", "out")
MLP_DVE = Steps("bn")

FILL = {
    0: [("post", 0, "hT"), ("pre", 0, "gates")], 1: [("post", 1, "hT"), ("pre", 1, "gates")],
    2: [("pre", 0, "in"), ("post", 0, "stats")], 3: [("pre", 0, "acc_in"), ("pre", 1, "in"), ("keep", 0, "keep")],
    4: [("pre", 0, "out"), ("pre", 1, "acc_in"), ("keep", 1, "keep")], 5: [("post", 1, "stats"), ("pre", 1, "out")],
    6: [("pre", 0, "y")], 7: [("pre", 1, "y")],
    8: [("pre", 0, "stats"), ("post", 0, "x2")], 9: [("pre", 1, "stats"), ("post", 1, "x2")],
    10: [("pre", 0, "x1"), ("post", 0, "agg")], 11: [("pre", 1, "x1"), ("post", 1, "agg")],
    12: [("pre", 0, "x1t"), ("post", 0, "w1a")], 13: [("pre", 1, "x1t"), ("post", 1, "w1a")],
    14: [("pre", 0, "xw0"), ("post", 0, "w1b")], 15: [("pre", 1, "xw0")], 16: [("pre", 0, "ax0"), ("post", 1, "w1b")],
    17: [("pre", 1, "ax0")], 18: [("pre", 0, "xw1")], 19: [("pre", 1, "xw1")], 20: [("pre", 0, "ax1")],
    21: [("pre", 1, "ax1")],
}
SHIFT = {"pre": 1, "keep": 0, "post": -1}

IN_PE, IN_ACT = Steps("zt"), Steps("z")
IN_DVE, IN_POOL = Steps("y", "stats", "aggr", "x3"), Steps("veps", "rstd", "keep")
QKV_PE, QKV_ACT, QKV_DVE = Steps("x3t", "q", "k", "v"), Steps("x3t", "q", "v"), Steps("k")
ATT_PE = Steps("sc0", "sc1", "sc2", "pt0", "sc3", "pt1", "pv0", "pt2", "pv1", "pt3", "pv2", "pv3")
ATT_ACT = Steps("exp0", "exp1", "pt0", "exp2", "pt1", "exp3", "pt2", "pt3")
ATT_DVE = Steps("m0", "max0", "m1", "max1", "m2", "max2", "m3", "max3")
ATT_POOL = Steps("sub0", "sub1", "sub2", "sub3")
OUT_DVE, OUT_POOL = Steps("rec", "att", "y", "stats", "aggr"), Steps("veps", "rstd", "out")


def exists(it):
    return not isinstance(it, int) or 0 <= it < NIT


def over(eng, body):
    for it in (-1, 0):
        body(it)
    with eng.Fori(1, NIT - 1) as it:
        body(it)
    for it in (NIT - 1, NIT):
        body(it)


def build(nc, t, out):
    x2_dram = nc.dram_tensor("x2_dram", (N, B, D), F32, kind="Internal").ap()

    with ExitStack() as top:
        def sb(name, shape, ctx=top):
            return ctx.enter_context(nc.sbuf_tensor(name, shape, F32))

        def sem(name, ctx=top):
            return ctx.enter_context(nc.semaphore(name))

        def flat(ap):
            return ap.rearrange("p a b -> p (a b)")

        bank = [top.enter_context(nc.psum_tensor(f"bank{k}", [128, 512], F32)) for k in range(8)]
        tile = [b[:].rearrange("p (g c) -> p g c", g=GB) for b in bank]

        agg_all = sb("agg_all", [128, B, N])
        ident = sb("ident", [128, 128])
        minus_half = sb("minus_half", [128, GB])
        w1T = sb("w1T", [128, H1 * 128])
        w2T = sb("w2T", [128, H1, 128])
        w3 = sb("w3", [128, 3 * D])
        mask = sb("mask", [128, 128])
        bn1_stats = sb("bn1_stats", [128, H1, NG, 6])
        bn2_stats = sb("bn2_stats", [128, NG, 6])
        bn1_par = sb("bn1_par", [128, 3, H1])
        bn2_par = sb("bn2_par", [128, 3])
        carrier = sem("carrier")
        consts_in = sem("consts_in")

        def settle(eng):
            eng.sem_inc(carrier, 1)

        with ExitStack() as one:
            def sb1(name, shape):
                return sb(name, shape, one)

            adj, adjT = sb1("adj", [128, 128]), sb1("adjT", [128, 128])
            w_inT, w_outT = sb1("w_inT", [128, 128]), sb1("w_outT", [128, 128])
            a_hatT = sb1("a_hatT", [128, 128])
            eb, oeb = sb1("eb", [128, 128]), sb1("oeb", [128, 128])
            gate_w, gate_b = sb1("gate_w", [128, 3]), sb1("gate_b", [128, 3])
            wg0, wg1 = sb1("wg0", [128, 128]), sb1("wg1", [128, 128])
            bg0, bg1 = sb1("bg0", [128, 128]), sb1("bg1", [128, 128])
            wihT, whhT = sb1("wihT", [128, MAXW, 512]), sb1("whhT", [128, MAXW, 512])
            bih, bhh, b_cell = (sb1(n, [128, MAXW * 4]) for n in ("bih", "bhh", "b_cell"))
            deg = sb1("deg", [128, 8])

            x_t = [sb1(f"x_t{s}", [128, GB, D]) for s in range(S)]
            x_f = [sb1(f"x_f{s}", [128, GB, N]) for s in range(S)]
            gz, sg = ([sb1(f"{n}{s}", [128, GB, 3]) for s in range(S)] for n in ("gz", "sg"))
            y1 = [sb1(f"y1_{s}", [128, GB, D]) for s in range(S)]
            x1 = [sb1(f"x1_{s}", [128, GB, D]) for s in range(S)]
            x1k = [sb1(f"x1k{s}", [128, GB, D]) for s in range(S)]
            x1T, xw, h1T, u_in, u_out = ([sb1(f"{n}{s}", [128, GB, D]) for s in range(S)] for n in ("x1T", "xw", "h1T", "u_in", "u_out"))
            hT = [sb1(f"hT{s}", [128, GB, N]) for s in range(S)]
            seq = [sb1(f"seq{s}", [128, GB, N]) for s in range(S)]
            hid = [sb1(f"hid{s}", [128, 256]) for s in range(S)]
            gi, gf, gg, go, ct, cc, ig = ([sb1(f"{n}{s}", [128, 256]) for s in range(S)]
                                          for n in ("gi", "gf", "gg", "go", "ct", "cc", "ig"))
            y2 = [sb1(f"y2_{s}", [128, GB, D]) for s in range(S)]
            x2 = [sb1(f"x2_{s}", [128, GB, D]) for s in range(S)]
            agg = [sb1(f"agg{s}", [128, GB, N]) for s in range(S)]
            ln_s = [sb1(f"ln_s{s}", [128, GB, 6]) for s in range(S)]
            ln_mv = [sb1(f"ln_mv{s}", [128, GB, 2]) for s in range(S)]
            ln_r = [sb1(f"ln_r{s}", [128, GB]) for s in range(S)]
            post_s = [sb1(f"post_s{s}", [128, GB, 6]) for s in range(S)]
            post_mv = [sb1(f"post_mv{s}", [128, GB, 2]) for s in range(S)]
            post_r = [sb1(f"post_r{s}", [128, GB]) for s in range(S)]

            with ExitStack() as zero:
                pool_set, dve_set, dve_link, pe_set = (sem(n, zero) for n in ("pool_set", "dve_set", "dve_link", "pe_set"))
                tmp, tmp2, origin, an = (sb(n, [128, 128], zero) for n in ("tmp", "tmp2", "origin", "an"))
                with nc.Block() as block:
                    loads = [(adj, t["adj"]), (adjT, t["adjT"]), (eb, t["eb"]), (oeb, t["oeb"]), (gate_w, t["gate_w"]),
                             (wg0, t["wg0"]), (wg1, t["wg1"]), (bg0, t["bg0"].partition_broadcast(128)),
                             (bg1, t["bg1"].partition_broadcast(128)), (wihT, t["wihT"]), (whhT, t["whhT"]),
                             (bih, t["bih"]), (bhh, t["bhh"]), (w1T, t["w1T"]), (w2T, t["w2T"]), (w3, t["w3"]),
                             (bn1_par, t["bn1"]), (bn2_par, t["bn2"])]

                    @block.sync
                    def _(sp):
                        for dst, src in loads:
                            sp.dma_start(dst[:], src).then_inc(consts_in, 16)
                        sp.dma_start(gate_b[:, 0:2], t["gate_b"]).then_inc(consts_in, 16)
                        sp.wait_ge(consts_in, 16 * (len(loads) + 1))

                    @block.gpsimd
                    def _(pool):
                        pool.memset(ident[:], 0.0).then_inc(pool_set, 1)
                        pool.memset(minus_half[:], -0.5).then_inc(pool_set, 1)
                        pool.wait_ge(pool_set, 2)
                        pool.affine_select(out=ident[:], in_=ident[:], compare_op=ALU.not_equal, fill=1.0, base=0,
                                           pattern=[[-1, 128]], channel_multiplier=1).then_inc(pool_set, 1)
                        pool.memset(gate_b[:, 2:3], 0.0).then_inc(pool_set, 1)
                        pool.wait_ge(dve_set, 11)
                        pool.tensor_tensor(deg[:, 4:5], deg[:, 3:4], minus_half[:, 0:1], ALU.pow).then_inc(pool_set, 1)

                    @block.vector
                    def _(dve):
                        done = [0]

                        def step(ins):
                            done[0] += 1
                            ins.then_inc(dve_set, 1)
                            dve.wait_ge(dve_set, done[0])

                        dve.wait_ge(consts_in, 16 * (len(loads) + 1))
                        dve.wait_ge(pool_set, 3)
                        step(nc.vector.tensor_scalar(tmp[:], adjT[:], 0.0, None, ALU.is_gt))
                        step(nc.vector.scalar_tensor_tensor(tmp2[:], adjT[:], 0.0, tmp[:], ALU.min, ALU.add))
                        step(nc.vector.tensor_tensor(w_inT[:], tmp2[:], adjT[:], ALU.mult))
                        step(nc.vector.tensor_scalar(tmp[:], adj[:], 0.0, None, ALU.is_gt))
                        step(nc.vector.scalar_tensor_tensor(origin[:], adj[:], 0.0, tmp[:], ALU.min, ALU.add))
                        step(nc.vector.tensor_tensor(w_outT[:], origin[:], adjT[:], ALU.mult))
                        step(nc.vector.tensor_tensor(an[:], adj[:], ident[:], ALU.add))
                        step(nc.vector.reduce_sum(deg[:, 0:1], an[:], AX))
                        step(nc.vector.tensor_tensor(tmp[:], adjT[:], ident[:], ALU.add))
                        step(nc.vector.tensor_tensor(tmp2[:], ident[:], an[:], ALU.mult))
                        nc.vector.reduce_sum(deg[:, 1:2], tmp[:], AX)
                        nc.vector.reduce_sum(deg[:, 2:3], tmp2[:], AX).then_inc(dve_link, 1)
                        dve.wait_ge(dve_link, 1)
                        nc.vector.tensor_tensor(deg[:, 5:6], deg[:, 1:2], deg[:, 2:3], ALU.subtract).then_inc(dve_link, 1)
                        dve.wait_ge(dve_link, 2)
                        step(nc.vector.tensor_tensor(deg[:, 3:4], deg[:, 0:1], deg[:, 5:6], ALU.add))
                        step(nc.vector.tensor_scalar(mask[:], adj[:], 0.0, MASKED, ALU.is_equal, ALU.mult))
                        step(nc.vector.tensor_tensor(b_cell[:], bih[:], bhh[:], ALU.add))
                        dve.wait_ge(pool_set, 5)
                        step(nc.vector.tensor_scalar(tmp[:], ident[:], deg[:, 4:5], None, ALU.mult))
                        dve.wait_ge(pe_set, 1)
                        step(nc.vector.tensor_scalar(a_hatT[:], bank[0][:, 0:128], deg[:, 4:5], None, ALU.mult))

                    @block.tensor
                    def _(pe):
                        pe.wait_ge(dve_set, 14)
                        pe.matmul(bank[0][:, 0:128], an[:], tmp[:], start=True, stop=True).then_inc(pe_set, 1)

            x_in = [sem(f"x_in{s}", one) for s in range(S)]
            x2_out = [sem(f"x2_out{s}", one) for s in range(S)]
            agg_out = [sem(f"agg_out{s}", one) for s in range(S)]
            pre_pe, pre_act, pre_dve, pre_pool, keep_pool, cell_pe, cell_act, cell_dve, post_pe, post_act, post_dve, post_pool = (
                [sem(f"{n}{s}", one) for s in range(S)]
                for n in ("pre_pe", "pre_act", "pre_dve", "pre_pool", "keep_pool", "cell_pe", "cell_act", "cell_dve",
                          "post_pe", "post_act", "post_dve", "post_pool"))
            PB = [bank[0], bank[1]]
            QB = [bank[2], bank[3]]
            PT, QT = [tile[0], tile[1]], [tile[2], tile[3]]
            GATE = [[bank[4], bank[5]], [bank[6], bank[7]]]

            def group(it, s):
                return bass.ds(it * (S * GB) + s * GB, GB)

            def body_of(unit, piece):
                def body(it):
                    def fill(k):
                        for stage, s, name in FILL[k]:
                            if exists(it + SHIFT[stage]):
                                piece(stage, it + SHIFT[stage], s, name)
                    for u in range(NU):
                        for s in range(S):
                            k = S * u + s
                            if exists(it):
                                unit(it, s, u, lambda k=k: fill(k))
                            else:
                                fill(k)
                return body

            with nc.Block() as block:
                @block.sync
                def _(sp):
                    for s in range(S):
                        sp.sem_inc(x2_out[s], 16)
                        sp.sem_inc(agg_out[s], 16)

                    def body(it):
                        if exists(it - 1):
                            for s in range(S):
                                sp.wait_ge(post_dve[s], POST_DVE.done(it - 1, "x2"))
                                settle(sp)
                                sp.dma_start(x2_dram[:, group(it - 1, s), :], x2[s][:]).then_inc(x2_out[s], 16)
                                sp.wait_ge(post_act[s], POST_ACT.done(it - 1, "agg"))
                                settle(sp)
                                sp.dma_start(agg_all[:, group(it - 1, s), :], agg[s][:]).then_inc(agg_out[s], 16)
                        if exists(it + 2):
                            for s in range(S):
                                sp.wait_ge(pre_dve[s], PRE_DVE.done_before(it + 2, "y"))
                                settle(sp)
                                sp.wait_ge(pre_pe[s], PRE_PE.done_before(it + 2, "gates"))
                                settle(sp)
                                sp.dma_start(x_t[s][:], t["x_t"][:, group(it + 2, s), :]).then_inc(x_in[s], 16)
                                sp.dma_start(x_f[s][:], t["x_f"][:, group(it + 2, s), :]).then_inc(x_in[s], 16)

                    for it in (-2, -1, 0):
                        body(it)
                    with sp.Fori(1, NIT - 2) as it:
                        body(it)
                    for it in (NIT - 2, NIT - 1, NIT):
                        body(it)
                    for s in range(S):
                        sp.wait_ge(agg_out[s], 16 * NIT + 16)
                        sp.wait_ge(x2_out[s], 16 * NIT + 16)

                @block.tensor
                def _(pe):
                    for s in range(S):
                        pe.sem_inc(pre_pe[s], PRE_PE.total)
                        pe.sem_inc(cell_pe[s], CELL_PE.total)
                        pe.sem_inc(post_pe[s], POST_PE.total)

                    def per_graph(dst, stationary, moving, transpose=False):
                        for b in range(GB):
                            if transpose:
                                last = pe.transpose(dst[:, b, :], stationary[:, b, :], ident[:])
                            else:
                                last = pe.matmul(dst[:, b, :], stationary[:, b, :], moving, start=True, stop=True)
                        return last

                    def pre(it, s, name):
                        if name == "gates":
                            pe.wait_ge(pre_act[s], PRE_ACT.done_before(it, "h2"))
                            pe.wait_ge(x_in[s], it * 32 + 32)
                            for b in range(GB):
                                last = pe.matmul(PB[s][:, 3 * b:3 * b + 3], x_f[s][:, b, :], gate_w[:], start=True, stop=True)
                            last.then_inc(pre_pe[s], 1)
                        elif name == "in":
                            pe.wait_ge(pre_dve[s], PRE_DVE.done(it, "gates"))
                            pe.matmul(PB[s][:], w_inT[:], flat(x_t[s][:]), start=True, stop=True).then_inc(pre_pe[s], 1)
                        elif name == "out":
                            pe.wait_ge(pre_dve[s], PRE_DVE.done(it, "in"))
                            pe.matmul(PB[s][:], w_outT[:], flat(x_t[s][:]), start=True, stop=True).then_inc(pre_pe[s], 1)
                        elif name == "x1t":
                            pe.wait_ge(pre_dve[s], PRE_DVE.done(it, "x1"))
                            per_graph(PT[s], x1[s], None, True).then_inc(pre_pe[s], 1)
                        elif name == "xw0":
                            pe.wait_ge(pre_act[s], PRE_ACT.done(it, "x1t"))
                            per_graph(PT[s], x1T[s], wg0[:]).then_inc(pre_pe[s], 1)
                        elif name == "ax0":
                            pe.wait_ge(pre_dve[s], PRE_DVE.done(it, "xw0"))
                            per_graph(PT[s], xw[s], adjT[:]).then_inc(pre_pe[s], 1)
                        elif name == "xw1":
                            pe.wait_ge(pre_act[s], PRE_ACT.done(it, "h1"))
                            per_graph(PT[s], h1T[s], wg1[:]).then_inc(pre_pe[s], 1)
                        elif name == "ax1":
                            pe.wait_ge(pre_dve[s], PRE_DVE.done(it, "xw1"))
                            per_graph(PT[s], xw[s], adjT[:]).then_inc(pre_pe[s], 1)

                    def cell(it, s, u, inside):
                        p, j, nw, b0, nb = UNITS[u]
                        n = nw * nb
                        if j == 0:
                            inside()
                        src = hT[s] if p == 1 else seq[s]
                        xs = src[:, b0:b0 + nb, bass.ds(j, nw, p)] if p > 1 else src[:, b0:b0 + nb, :]
                        slot = {GI: GATE[s][0][:, 0:n], GG: GATE[s][0][:, 256:256 + n],
                                GF: GATE[s][1][:, 0:n], GO: GATE[s][1][:, 256:256 + n]}

                        def out3(g):
                            return slot[g].rearrange("p (b w) -> p b w", b=nb)

                        def wx(g):
                            return wihT[:, p - 1, g * 128:(g + 1) * 128]

                        def wh(g):
                            return whhT[:, p - 1, g * 128:(g + 1) * 128]

                        if u == 0:
                            pe.wait_ge(pre_act[s], PRE_ACT.done(it, "h2"))
                            pe.wait_ge(cell_act[s], CELL_ACT.done_before(it, f"{NU - 1}o"))
                        elif j or p == 1:
                            pe.wait_ge(cell_act[s], CELL_ACT.done(it, f"{u - 1}o"))
                        else:
                            pe.wait_ge(cell_dve[s], CELL_DVE.done(it, f"{u - 1}h"))
                        if j == 0:
                            pe.matmul(out3(GI), wx(GI), xs, start=True, stop=True)
                            pe.matmul(out3(GG), wx(GG), xs, start=True, stop=True).then_inc(cell_pe[s], 1)
                            pe.matmul(out3(GO), wx(GO), xs, start=True, stop=True).then_inc(cell_pe[s], 1)
                            return
                        hs = hid[s][:, 0:n]
                        for k, g in enumerate((GI, GG, GF, GO)):
                            pe.matmul(out3(g), wx(g), xs, start=(k % 2 == 0), stop=False, skip_group_check=True)
                        inside()
                        pe.wait_ge(cell_dve[s], CELL_DVE.done(it, f"{u - 1}h"))
                        for k, g in enumerate((GI, GG, GF, GO)):
                            last = pe.matmul(slot[g], wh(g), hs, start=False, stop=True, skip_group_check=True)
                            if k % 2:
                                last.then_inc(cell_pe[s], 1)

                    def post(it, s, name):
                        if name == "hT":
                            pe.wait_ge(cell_dve[s], CELL_DVE.done(it, f"{NU - 1}h"))
                            pe.wait_ge(post_dve[s], POST_DVE.done_before(it, "bnb"))
                            per_graph(QT[s], seq[s], None, True).then_inc(post_pe[s], 1)
                        elif name == "agg":
                            pe.wait_ge(post_dve[s], POST_DVE.done(it, "x2"))
                            per_graph(QT[s], x2[s], a_hatT[:]).then_inc(post_pe[s], 1)
                        elif name == "w1a":
                            pe.wait_ge(post_act[s], POST_ACT.done(it, "agg"))
                            pe.matmul(QB[s][:], w1T[:, 0:128], flat(agg[s][:]), start=True, stop=True).then_inc(post_pe[s], 1)
                        elif name == "w1b":
                            pe.wait_ge(post_dve[s], POST_DVE.done(it, "bna"))
                            pe.matmul(QB[s][:], w1T[:, 128:256], flat(agg[s][:]), start=True, stop=True).then_inc(post_pe[s], 1)

                    def piece(stage, it, s, name):
                        if stage != "keep":
                            (pre if stage == "pre" else post)(it, s, name)

                    over(pe, body_of(cell, piece))

                @block.scalar
                def _(act):
                    for s in range(S):
                        act.sem_inc(pre_act[s], PRE_ACT.total)
                        act.sem_inc(cell_act[s], CELL_ACT.total)
                        act.sem_inc(post_act[s], POST_ACT.total)

                    def piece(stage, it, s, name):
                        if name == "gates":
                            act.wait_ge(pre_dve[s], PRE_DVE.done(it, "gates"))
                            act.activation(sg[s][:], gz[s][:], ACT.Sigmoid).then_inc(pre_act[s], 1)
                        elif name == "in":
                            act.wait_ge(pre_act[s], PRE_ACT.done(it, "gates"))
                            for b in range(GB):
                                last = act.activation(y1[s][:, b, :], x_t[s][:, b, :], ACT.Copy, scale=sg[s][:, b, 2:3])
                            last.then_inc(pre_act[s], 1)
                        elif name == "x1t":
                            act.wait_ge(pre_pe[s], PRE_PE.done(it, "x1t"))
                            act.activation(x1T[s][:], PT[s], ACT.Copy).then_inc(pre_act[s], 1)
                        elif name == "ax0":
                            act.wait_ge(pre_pe[s], PRE_PE.done(it, "ax0"))
                            act.activation(h1T[s][:], PT[s], ACT.Relu).then_inc(pre_act[s], 1)
                        elif name == "ax1":
                            act.wait_ge(pre_pe[s], PRE_PE.done(it, "ax1"))
                            act.activation(hT[s][:], PT[s], ACT.Relu).then_inc(pre_act[s], 1)
                        elif name == "agg":
                            act.wait_ge(agg_out[s], it * 16 + 16)
                            act.wait_ge(post_pe[s], POST_PE.done(it, "agg"))
                            act.activation(agg[s][:], QT[s], ACT.Copy).then_inc(post_act[s], 1)

                    def cell(it, s, u, inside):
                        p, j, nw, b0, nb = UNITS[u]
                        n = nw * nb

                        def gate(dst, g, func):
                            k, at = {GI: (0, 0), GG: (0, 256), GF: (1, 0), GO: (1, 256)}[g]
                            col = 4 * (p - 1) + g
                            act.activation(dst[s][:, 0:n], GATE[s][k][:, at:at + n], func,
                                           bias=b_cell[:, col:col + 1]).then_inc(cell_act[s], 1)

                        act.wait_ge(cell_pe[s], CELL_PE.done(it, f"{u}ig"))
                        gate(gi, GI, ACT.Sigmoid)
                        gate(gg, GG, ACT.Tanh)
                        act.wait_ge(cell_pe[s], CELL_PE.done(it, f"{u}fo"))
                        if j:
                            gate(gf, GF, ACT.Sigmoid)
                        if u == 1:
                            act.wait_ge(cell_dve[s], CELL_DVE.done(it, "0h"))
                        if u == 0:
                            act.wait_ge(cell_dve[s], CELL_DVE.done_before(it, f"{NU - 1}h"))
                        gate(go, GO, ACT.Sigmoid)
                        inside()
                        act.wait_ge(cell_dve[s], CELL_DVE.done(it, f"{u}c"))
                        act.activation(ct[s][:, 0:n], cc[s][:, 0:n], ACT.Tanh).then_inc(cell_act[s], 1)

                    over(act, body_of(cell, piece))

                @block.vector
                def _(dve):
                    for s in range(S):
                        dve.sem_inc(pre_dve[s], PRE_DVE.total)
                        dve.sem_inc(cell_dve[s], CELL_DVE.total)
                        dve.sem_inc(post_dve[s], POST_DVE.total)

                    def pre(it, s, name):
                        def own(step):
                            dve.wait_ge(pre_dve[s], PRE_DVE.done(it, step))

                        def wide(m):
                            return m[:].unsqueeze(1).broadcast_to([128, GB, m.shape[-1]])

                        if name == "gates":
                            dve.wait_ge(pre_pe[s], PRE_PE.done(it, "gates"))
                            dve.tensor_tensor(gz[s][:], PB[s][:, 0:3 * GB].rearrange("p (b g) -> p b g", g=3), wide(gate_b),
                                              ALU.add).then_inc(pre_dve[s], 1)
                        elif name == "in":
                            dve.wait_ge(pre_pe[s], PRE_PE.done(it, "in"))
                            dve.tensor_tensor(u_in[s][:], PT[s], wide(eb), ALU.add).then_inc(pre_dve[s], 1)
                        elif name == "out":
                            dve.wait_ge(pre_pe[s], PRE_PE.done(it, "out"))
                            dve.tensor_tensor(u_out[s][:], PT[s], wide(oeb), ALU.add).then_inc(pre_dve[s], 1)
                        elif name == "acc_in":
                            own("in")
                            dve.wait_ge(pre_act[s], PRE_ACT.done(it, "loop"))
                            for b in range(GB):
                                last = dve.scalar_tensor_tensor(y1[s][:, b, :], u_in[s][:, b, :], sg[s][:, b, 0:1],
                                                                y1[s][:, b, :], ALU.mult, ALU.add)
                            last.then_inc(pre_dve[s], 1)
                        elif name == "y":
                            own("out")
                            for b in range(GB):
                                last = dve.scalar_tensor_tensor(y1[s][:, b, :], u_out[s][:, b, :], sg[s][:, b, 1:2],
                                                                y1[s][:, b, :], ALU.mult, ALU.add)
                            last.then_inc(pre_dve[s], 1)
                            own("acc_out")
                            dve.scalar_tensor_tensor(y1[s][:], y1[s][:], 0.0, x_t[s][:], ALU.max, ALU.add).then_inc(pre_dve[s], 1)
                        elif name == "stats":
                            own("y")
                            settle(dve)
                            for b in range(GB):
                                last = dve.bn_stats(ln_s[s][:, b, :], y1[s][:, b, :])
                            last.then_inc(pre_dve[s], 1)
                            own("stats")
                            settle(dve)
                            for b in range(GB):
                                last = dve.bn_aggr(ln_mv[s][:, b, :], ln_s[s][:, b, :])
                            last.then_inc(pre_dve[s], 1)
                        elif name == "x1":
                            dve.wait_ge(keep_pool[s], KEEP.done_before(it, "keep"))
                            dve.wait_ge(pre_pool[s], PRE_POOL.done(it, "rstd"))
                            settle(dve)
                            for b in range(GB):
                                last = dve.tensor_scalar(x1[s][:, b, :], y1[s][:, b, :], ln_mv[s][:, b, 0:1],
                                                         ln_r[s][:, b:b + 1], ALU.subtract, ALU.mult)
                            last.then_inc(pre_dve[s], 1)
                        elif name in ("xw0", "xw1"):
                            dve.wait_ge(pre_pe[s], PRE_PE.done(it, name))
                            dve.tensor_tensor(xw[s][:], PT[s], wide(bg0 if name == "xw0" else bg1), ALU.add).then_inc(pre_dve[s], 1)

                    def cell(it, s, u, inside):
                        p, j, nw, b0, nb = UNITS[u]
                        n = nw * nb
                        a, b, c, d = (x[s][:, 0:n] for x in (gi, gg, cc, ig))
                        dve.wait_ge(cell_act[s], CELL_ACT.done(it, f"{u}g"))
                        dve.tensor_tensor(c if j == 0 else d, a, b, ALU.mult).then_inc(cell_dve[s], 1)
                        if j:
                            dve.wait_ge(cell_act[s], CELL_ACT.done(it, f"{u}f"))
                            dve.tensor_tensor(c, gf[s][:, 0:n], c, ALU.mult).then_inc(cell_dve[s], 1)
                            dve.wait_ge(cell_dve[s], CELL_DVE.done(it, f"{u}fc"))
                            dve.tensor_tensor(c, c, d, ALU.add).then_inc(cell_dve[s], 1)
                        inside()
                        if u == 0:
                            dve.wait_ge(post_pe[s], POST_PE.done_before(it, "hT"))
                        dve.wait_ge(cell_act[s], CELL_ACT.done(it, f"{u}t"))
                        if j == p - 1:
                            o = seq[s][:, b0:b0 + nb, bass.ds(j, nw, p)] if p > 1 else seq[s][:, b0:b0 + nb, :]
                        else:
                            o = hid[s][:, 0:n].rearrange("p (b w) -> p b w", b=nb)
                        dve.tensor_tensor(o, go[s][:, 0:n].rearrange("p (b w) -> p b w", b=nb),
                                          ct[s][:, 0:n].rearrange("p (b w) -> p b w", b=nb), ALU.mult).then_inc(cell_dve[s], 1)

                    def post(it, s, name):
                        def own(step):
                            dve.wait_ge(post_dve[s], POST_DVE.done(it, step))
                            settle(dve)

                        if name == "hT":
                            dve.wait_ge(keep_pool[s], KEEP.done(it, "keep"))
                            dve.wait_ge(post_pe[s], POST_PE.done(it, "hT"))
                            dve.tensor_tensor(y2[s][:], QT[s], x1k[s][:], ALU.add).then_inc(post_dve[s], 1)
                        elif name == "stats":
                            own("y")
                            for b in range(GB):
                                last = dve.bn_stats(post_s[s][:, b, :], y2[s][:, b, :])
                            last.then_inc(post_dve[s], 1)
                            own("stats")
                            for b in range(GB):
                                last = dve.bn_aggr(post_mv[s][:, b, :], post_s[s][:, b, :])
                            last.then_inc(post_dve[s], 1)
                        elif name == "x2":
                            dve.wait_ge(x2_out[s], it * 16 + 16)
                            dve.wait_ge(post_pool[s], POST_POOL.done(it, "rstd"))
                            settle(dve)
                            for b in range(GB):
                                last = dve.tensor_scalar(x2[s][:, b, :], y2[s][:, b, :], post_mv[s][:, b, 0:1],
                                                         post_r[s][:, b:b + 1], ALU.subtract, ALU.mult)
                            last.then_inc(post_dve[s], 1)
                        elif name in ("w1a", "w1b"):
                            dve.wait_ge(post_pe[s], POST_PE.done(it, name))
                            settle(dve)
                            stats = bn1_stats[:, int(name == "w1b"), bass.ds(it * S + s, 1), :]
                            dve.bn_stats(stats.rearrange("p a b -> p (a b)"), QB[s][:]).then_inc(post_dve[s], 1)

                    def piece(stage, it, s, name):
                        if stage != "keep":
                            (pre if stage == "pre" else post)(it, s, name)

                    over(dve, body_of(cell, piece))

                @block.gpsimd
                def _(pool):
                    for s in range(S):
                        pool.sem_inc(pre_pool[s], PRE_POOL.total)
                        pool.sem_inc(keep_pool[s], KEEP.total)
                        pool.sem_inc(post_pool[s], POST_POOL.total)

                    def rstd(r, mv, done, steps, it):
                        settle(pool)
                        pool.tensor_scalar(r[:], mv[:, :, 1], EPS, None, ALU.add).then_inc(done, 1)
                        pool.wait_ge(done, steps.done(it, "veps"))
                        pool.tensor_tensor(r[:], r[:], minus_half[:], ALU.pow).then_inc(done, 1)

                    def piece(stage, it, s, name):
                        if stage == "pre" and name == "stats":
                            pool.wait_ge(pre_dve[s], PRE_DVE.done(it, "aggr"))
                            rstd(ln_r[s], ln_mv[s], pre_pool[s], PRE_POOL, it)
                        elif name == "stats":
                            pool.wait_ge(post_dve[s], POST_DVE.done(it, "aggr"))
                            rstd(post_r[s], post_mv[s], post_pool[s], POST_POOL, it)
                        elif name == "keep":
                            pool.wait_ge(post_dve[s], POST_DVE.done_before(it, "y"))
                            settle(pool)
                            pool.wait_ge(pre_dve[s], PRE_DVE.done(it, "x1"))
                            settle(pool)
                            pool.tensor_copy(x1k[s][:], x1[s][:]).then_inc(keep_pool[s], 1)

                    over(pool, body_of(lambda it, s, u, inside: inside(), piece))

        bn1_mv = sb("bn1_mv", [128, H1, 2])
        bn1_scale, bn1_shift = sb("bn1_scale", [128, H1]), sb("bn1_shift", [128, H1])
        bn2_mv = sb("bn2_mv", [128, 2])
        bn2_scale, bn2_shift = sb("bn2_scale", [128, 1]), sb("bn2_shift", [128, 1])
        bn_tmp = sb("bn_tmp", [128, 2 * H1])

        def bn_dve(dve, s_dve, s_pool, n, stats, mv, b, g, be, scale, shift):
            count = [0]

            def step(ins):
                ins.then_inc(s_dve, 1)
                count[0] += 1
                dve.wait_ge(s_dve, count[0])
            for k in range(n):
                step(dve.bn_aggr(mv[k], stats[k]))
            mean_ap = bn_mean(mv, n)
            step(dve.tensor_tensor(bn_tmp[:, 0:n], mean_ap, b, ALU.add))
            step(dve.tensor_tensor(bn_tmp[:, n:2 * n], b, bn_tmp[:, 0:n], ALU.subtract))
            dve.wait_ge(s_pool, 2)
            step(dve.tensor_tensor(scale, scale, g, ALU.mult))
            step(dve.tensor_tensor(bn_tmp[:, 0:n], bn_tmp[:, n:2 * n], scale, ALU.mult))
            step(dve.tensor_tensor(shift, bn_tmp[:, 0:n], be, ALU.add))
            return count[0]

        def bn_mean(mv, n):
            return bn1_mv[:, :, 0] if n == H1 else bn2_mv[:, 0:1]

        def bn_pool(pool, s_dve, s_pool, n, var, scale):
            pool.wait_ge(s_dve, n)
            pool.tensor_scalar(scale, var, EPS, None, ALU.add).then_inc(s_pool, 1)
            pool.wait_ge(s_pool, 1)
            pool.tensor_tensor(scale, scale, minus_half[:, 0:n], ALU.pow).then_inc(s_pool, 1)

        with ExitStack() as two:
            bn1_dve, bn1_pool = sem("bn1_dve", two), sem("bn1_pool", two)
            mlp_pe, mlp_act, mlp_dve = ([sem(f"{n}{s}", two) for s in range(S)] for n in ("mlp_pe", "mlp_act", "mlp_dve"))
            hid1 = [sb(f"hid1_{s}", [128, H1, C], two) for s in range(S)]
            BN1_DONE = H1 + 5
            W1B = [[bank[0], bank[1]], [bank[2], bank[3]]]
            W2B = [bank[4], bank[5]]

            with nc.Block() as block:
                def cols(it, s):
                    return agg_all[:, bass.ds(it * (S * GB) + s * GB, GB), :]

                @block.gpsimd
                def _(pool):
                    bn_pool(pool, bn1_dve, bn1_pool, H1, bn1_mv[:, :, 1], bn1_scale[:])

                @block.tensor
                def _(pe):
                    for s in range(S):
                        pe.sem_inc(mlp_pe[s], MLP_PE.total)

                    with pe.Fori(0, NIT) as it:
                        for s in range(S):
                            for h in range(H1):
                                pe.wait_ge(mlp_act[s], MLP_ACT.done_before(it, f"h{h}"))
                                settle(pe)
                                pe.matmul(W1B[s][h][:], w1T[:, h * 128:(h + 1) * 128], cols(it, s), start=True,
                                          stop=True).then_inc(mlp_pe[s], 1)
                        for s in range(S):
                            pe.wait_ge(mlp_act[s], MLP_ACT.done_before(it, "out"))
                            pe.wait_ge(mlp_dve[s], MLP_DVE.done_before(it, "bn"))
                            for h in range(H1):
                                pe.wait_ge(mlp_act[s], MLP_ACT.done(it, f"h{h}"))
                                last = pe.matmul(W2B[s][:], w2T[:, h, :], hid1[s][:, h, :], start=(h == 0),
                                                 stop=(h == H1 - 1))
                            last.then_inc(mlp_pe[s], 1)

                @block.scalar
                def _(act):
                    for s in range(S):
                        act.sem_inc(mlp_act[s], MLP_ACT.total)
                    act.wait_ge(bn1_dve, BN1_DONE)
                    with act.Fori(0, NIT) as it:
                        for s in range(S):
                            for h, name in enumerate(("w1a", "w1b")):
                                act.wait_ge(mlp_pe[s], MLP_PE.done(it, name))
                                act.activation(hid1[s][:, h, :], W1B[s][h][:], ACT.Relu, bias=bn1_shift[:, h:h + 1],
                                               scale=bn1_scale[:, h:h + 1]).then_inc(mlp_act[s], 1)
                        for s in range(S):
                            act.wait_ge(mlp_dve[s], MLP_DVE.done(it, "bn"))
                            settle(act)
                            act.activation(cols(it, s), W2B[s][:].rearrange("p (b n) -> p b n", b=GB),
                                           ACT.Copy).then_inc(mlp_act[s], 1)

                @block.vector
                def _(dve):
                    for s in range(S):
                        dve.sem_inc(mlp_dve[s], MLP_DVE.total)
                    n = bn_dve(dve, bn1_dve, bn1_pool, H1, [bn1_stats[:, h, :, :].rearrange("p a b -> p (a b)") for h in range(H1)],
                               [bn1_mv[:, h, :] for h in range(H1)], bn1_par[:, 0, :], bn1_par[:, 1, :], bn1_par[:, 2, :],
                               bn1_scale[:], bn1_shift[:])
                    assert n == BN1_DONE
                    with dve.Fori(0, NIT) as it:
                        for s in range(S):
                            dve.wait_ge(mlp_pe[s], MLP_PE.done(it, "w2"))
                            settle(dve)
                            dve.bn_stats(bn2_stats[:, bass.ds(it * S + s, 1), :].rearrange("p a b -> p (a b)"),
                                         W2B[s][:]).then_inc(mlp_dve[s], 1)

        with ExitStack() as three:
            def sb3(name, shape):
                return sb(name, shape, three)

            bn2_dve, bn2_pool = sem("bn2_dve", three), sem("bn2_pool", three)
            ones_set = sem("ones_set", three)
            x2_in, out_done = ([sem(f"{n}{s}", three) for s in range(S)] for n in ("x2_in", "out_done"))
            in_pe, in_act, in_dve, in_pool, qkv_pe, qkv_act, qkv_dve, att_pe, att_act, att_dve, att_pool, out_dve, out_pool = (
                [sem(f"{n}{s}", three) for s in range(S)]
                for n in ("in_pe", "in_act", "in_dve", "in_pool", "qkv_pe", "qkv_act", "qkv_dve",
                          "att_pe", "att_act", "att_dve", "att_pool", "out_dve", "out_pool"))
            x2b = [sb3(f"x2b{s}", [128, GB, D]) for s in range(S)]
            z, ya, yc, x3, x3k, x3T, qT, kT, fin = ([sb3(f"{n}{s}", [128, GB, D]) for s in range(S)]
                                                    for n in ("z", "ya", "yc", "x3_", "x3k", "x3T", "qT", "kT", "fin"))
            v = [sb3(f"v{s}", [128, GB, NH, HD + 1]) for s in range(S)]
            pr = [[sb3(f"pr{s}{h}", [128, GB, N]) for h in range(NH)] for s in range(S)]
            prT = [sb3(f"prT{k}", [128, GB, N]) for k in range(2)]
            mx = [sb3(f"mx{s}", [128, NH, GB]) for s in range(S)]
            rec = [sb3(f"rec{s}", [128, GB, NH]) for s in range(S)]
            in_s, out_s = ([sb3(f"{n}{s}", [128, GB, 6]) for s in range(S)] for n in ("in_s", "out_s"))
            in_mv, out_mv = ([sb3(f"{n}{s}", [128, GB, 2]) for s in range(S)] for n in ("in_mv", "out_mv"))
            in_r, out_r = ([sb3(f"{n}{s}", [128, GB]) for s in range(S)] for n in ("in_r", "out_r"))
            GT, GK = [tile[0], tile[1]], [bank[0], bank[1]]
            ST = [tile[2], tile[3]]
            PTB = [tile[4], tile[5]]
            OB = [bank[6 + k][:, 0:2 * NH * (HD + 1)].rearrange("p (b h e) -> p b h e", b=2, h=NH) for k in range(2)]
            BN2_DONE = 1 + 5
            SCALE = float(1.0 / HD ** 0.5)

            def group3(it, s):
                return bass.ds(it * (S * GB) + s * GB, GB)

            def shift(it, s, n):
                return it + (s + n) // S, (s + n) % S

            def halves(slot):
                def body(it):
                    for s in range(S):
                        for h in range(NH):
                            slot(it, s, h)
                return body

            def each(it, s, n, piece, *args):
                jt, js = shift(it, s, n)
                if exists(jt):
                    piece(jt, js, *args)

            def head(it, s, h, lag, piece):
                n = (h - lag) // NH
                each(it, s, n, piece, (h - lag) % NH)

            with nc.Block() as block:
                @block.sync
                def _(sp):
                    for s in range(S):
                        sp.sem_inc(out_done[s], 16)

                    def load(it, s):
                        sp.wait_ge(in_dve[s], IN_DVE.done_before(it, "y"))
                        settle(sp)
                        sp.dma_start(x2b[s][:], x2_dram[:, group3(it, s), :]).then_inc(x2_in[s], 16)

                    def store(it, s):
                        sp.wait_ge(out_pool[s], OUT_POOL.done(it, "out"))
                        settle(sp)
                        sp.dma_start(out[:, group3(it, s), :], fin[s][:]).then_inc(out_done[s], 16)

                    def body(it):
                        for s in range(S):
                            each(it, s, -2, store)
                            each(it, s, 4, load)

                    for it in (-2, -1, 0):
                        body(it)
                    with sp.Fori(1, NIT - 2) as it:
                        body(it)
                    for it in (NIT - 2, NIT - 1, NIT):
                        body(it)
                    for s in range(S):
                        sp.wait_ge(out_done[s], 16 * NIT + 16)

                @block.gpsimd
                def _(pool):
                    for s in range(S):
                        pool.sem_inc(in_pool[s], IN_POOL.total)
                        pool.sem_inc(att_pool[s], ATT_POOL.total)
                        pool.sem_inc(out_pool[s], OUT_POOL.total)
                        pool.memset(v[s][:, :, :, HD:HD + 1], 1.0).then_inc(ones_set, 1)
                    bn_pool(pool, bn2_dve, bn2_pool, 1, bn2_mv[:, 1:2], bn2_scale[:])

                    def rstd(r, mv, done, steps, it):
                        settle(pool)
                        pool.tensor_scalar(r[:], mv[:, :, 1], EPS, None, ALU.add).then_inc(done, 1)
                        pool.wait_ge(done, steps.done(it, "veps"))
                        pool.tensor_tensor(r[:], r[:], minus_half[:], ALU.pow).then_inc(done, 1)

                    def sub(it, s, h):
                        pool.wait_ge(att_dve[s], ATT_DVE.done(it, f"max{h}"))
                        pool.tensor_tensor(pr[s][h][:], pr[s][h][:], mx[s][:, h, :].unsqueeze(2).broadcast_to([128, GB, N]),
                                           ALU.subtract).then_inc(att_pool[s], 1)

                    def in_norm(it, s):
                        pool.wait_ge(in_dve[s], IN_DVE.done(it, "aggr"))
                        rstd(in_r[s], in_mv[s], in_pool[s], IN_POOL, it)

                    def keep(it, s):
                        pool.wait_ge(out_dve[s], OUT_DVE.done_before(it, "y"))
                        settle(pool)
                        pool.wait_ge(in_dve[s], IN_DVE.done(it, "x3"))
                        settle(pool)
                        pool.tensor_copy(x3k[s][:], x3[s][:]).then_inc(in_pool[s], 1)

                    def last_norm(it, s):
                        pool.wait_ge(out_dve[s], OUT_DVE.done(it, "aggr"))
                        rstd(out_r[s], out_mv[s], out_pool[s], OUT_POOL, it)
                        pool.wait_ge(out_done[s], it * 16 + 16)
                        settle(pool)
                        pool.wait_ge(out_pool[s], OUT_POOL.done(it, "rstd"))
                        settle(pool)
                        for b in range(GB):
                            last = pool.tensor_scalar(fin[s][:, b, :], yc[s][:, b, :], out_mv[s][:, b, 0:1],
                                                      out_r[s][:, b:b + 1], ALU.subtract, ALU.mult)
                        last.then_inc(out_pool[s], 1)

                    def slot(it, s, h):
                        if h == 2:
                            each(it, s, 0, keep)
                            each(it, s, 2, in_norm)
                        each(it, s, 0, sub, h)
                        if h == 1:
                            each(it, s, -2, last_norm)

                    over(pool, halves(slot))

                @block.tensor
                def _(pe):
                    for sems, steps in ((in_pe, IN_PE), (qkv_pe, QKV_PE), (att_pe, ATT_PE)):
                        for s in range(S):
                            pe.sem_inc(sems[s], steps.total)

                    def turn_tile(dst, src):
                        for b in range(GB):
                            last = pe.transpose(dst[:, b, :], src[:, b, :], ident[:])
                        return last

                    def other(it, s, sems, steps, name):
                        if s:
                            pe.wait_ge(sems[0], steps.done(it, name))
                        else:
                            pe.wait_ge(sems[1], steps.done_before(it, name))

                    def zt(it, s):
                        pe.wait_ge(qkv_dve[s], QKV_DVE.done_before(it, "k"))
                        pe.wait_ge(in_act[s], IN_ACT.done(it, "z"))
                        turn_tile(GT[0], z[s]).then_inc(in_pe[s], 1)

                    def x3t(it, s):
                        other(it, s, qkv_act, QKV_ACT, "v")
                        pe.wait_ge(in_dve[s], IN_DVE.done(it, "x3"))
                        turn_tile(GT[1], x3[s]).then_inc(qkv_pe[s], 1)

                    def q(it, s):
                        pe.wait_ge(qkv_act[s], QKV_ACT.done(it, "x3t"))
                        pe.matmul(GK[1][:], w3[:, 0:D], flat(x3T[s][:]), start=True, stop=True).then_inc(qkv_pe[s], 1)

                    def k(it, s):
                        if s:
                            if exists(it + 1):
                                pe.wait_ge(in_dve[0], IN_DVE.done(it + 1, "y"))
                            else:
                                pe.wait_ge(qkv_dve[0], QKV_DVE.done(it, "k"))
                        else:
                            pe.wait_ge(in_dve[1], IN_DVE.done(it, "y"))
                        pe.matmul(GK[0][:], w3[:, D:2 * D], flat(x3T[s][:]), start=True, stop=True).then_inc(qkv_pe[s], 1)

                    def vee(it, s):
                        pe.wait_ge(qkv_act[s], QKV_ACT.done(it, "q"))
                        for b in range(GB):
                            last = pe.matmul(GT[1][:, b, :], x3T[s][:, b, :], w3[:, 2 * D:3 * D], start=True, stop=True)
                        last.then_inc(qkv_pe[s], 1)

                    def scores(it, s, h):
                        if h == 0:
                            pe.wait_ge(qkv_dve[s], QKV_DVE.done(it, "k"))
                        if h < 2:
                            other(it, s, att_dve, ATT_DVE, f"m{h + 2}")
                        else:
                            pe.wait_ge(att_dve[s], ATT_DVE.done(it, f"m{h - 2}"))
                        for b in range(GB):
                            last = pe.matmul(ST[h % 2][:, b, :], qT[s][h * HD:(h + 1) * HD, b, :],
                                             kT[s][h * HD:(h + 1) * HD, b, :], start=True, stop=True)
                        last.then_inc(att_pe[s], 1)

                    def turn(it, s, h):
                        if h < 2:
                            other(it, s, att_act, ATT_ACT, f"pt{h + 2}")
                        pe.wait_ge(att_act[s], ATT_ACT.done(it, f"exp{h}"))
                        turn_tile(PTB[h % 2], pr[s][h]).then_inc(att_pe[s], 1)

                    def values(it, s, h):
                        if h == 0:
                            other(it, s, out_dve, OUT_DVE, "att")
                            pe.wait_ge(qkv_act[s], QKV_ACT.done(it, "v"))
                        pe.wait_ge(att_act[s], ATT_ACT.done(it, f"pt{h}"))
                        for b in range(GB):
                            last = pe.matmul(OB[b // 2][:, b % 2, h, :], prT[h % 2][:, b, :], v[s][:, b, h, :],
                                             start=True, stop=True)
                        last.then_inc(att_pe[s], 1)

                    def slot(it, s, h):
                        each(it, s, 0, scores, h)
                        head(it, s, h, 2, turn)
                        head(it, s, h, 3, values)
                        if h == 1:
                            each(it, s, 2, zt)
                        each(it, s, 1, (x3t, q, k, vee)[h])

                    pe.wait_ge(ones_set, S)
                    over(pe, halves(slot))

                @block.scalar
                def _(act):
                    for sems, steps in ((in_act, IN_ACT), (qkv_act, QKV_ACT), (att_act, ATT_ACT)):
                        for s in range(S):
                            act.sem_inc(sems[s], steps.total)
                    act.wait_ge(bn2_dve, BN2_DONE)

                    def batch_norm(it, s):
                        act.wait_ge(in_pe[s], IN_PE.done_before(it, "zt"))
                        settle(act)
                        act.activation(z[s][:], agg_all[:, group3(it, s), :], ACT.Identity, bias=bn2_shift[:, 0:1],
                                       scale=bn2_scale[:, 0:1]).then_inc(in_act[s], 1)

                    def x3t(it, s):
                        act.wait_ge(qkv_pe[s], QKV_PE.done(it, "x3t"))
                        act.activation(x3T[s][:], GT[1], ACT.Copy).then_inc(qkv_act[s], 1)

                    def q(it, s):
                        act.wait_ge(qkv_pe[s], QKV_PE.done(it, "q"))
                        act.activation(qT[s][:], GT[1], ACT.Copy).then_inc(qkv_act[s], 1)

                    def vee(it, s):
                        act.wait_ge(qkv_pe[s], QKV_PE.done(it, "v"))
                        act.activation(v[s][:, :, :, 0:HD], GT[1].rearrange("p b (h e) -> p b h e", h=NH),
                                       ACT.Copy).then_inc(qkv_act[s], 1)

                    def exp(it, s, h):
                        act.wait_ge(att_pool[s], ATT_POOL.done(it, f"sub{h}"))
                        act.activation(pr[s][h][:], pr[s][h][:], ACT.Exp).then_inc(att_act[s], 1)

                    def turned(it, s, h):
                        act.wait_ge(att_pe[s], ATT_PE.done(it, f"pt{h}"))
                        act.activation(prT[h % 2][:], PTB[h % 2], ACT.Copy).then_inc(att_act[s], 1)

                    def slot(it, s, h):
                        head(it, s, h, 1, exp)
                        head(it, s, h, 2, turned)
                        if h == 0:
                            each(it, s, 2, batch_norm)
                            each(it, s, 1, x3t)
                        if h == 1:
                            each(it, s, 1, q)
                        if h == 3:
                            each(it, s, 1, vee)

                    over(act, halves(slot))

                @block.vector
                def _(dve):
                    for sems, steps in ((in_dve, IN_DVE), (qkv_dve, QKV_DVE), (att_dve, ATT_DVE), (out_dve, OUT_DVE)):
                        for s in range(S):
                            dve.sem_inc(sems[s], steps.total)
                    n = bn_dve(dve, bn2_dve, bn2_pool, 1, [bn2_stats[:].rearrange("p a b -> p (a b)")], [bn2_mv[:]],
                               bn2_par[:, 0:1], bn2_par[:, 1:2], bn2_par[:, 2:3], bn2_scale[:], bn2_shift[:])
                    assert n == BN2_DONE

                    def norm_stats(it, y, st, mv, done, steps):
                        dve.wait_ge(done, steps.done(it, "y"))
                        settle(dve)
                        for b in range(GB):
                            last = dve.bn_stats(st[:, b, :], y[:, b, :])
                        last.then_inc(done, 1)
                        dve.wait_ge(done, steps.done(it, "stats"))
                        settle(dve)
                        for b in range(GB):
                            last = dve.bn_aggr(mv[:, b, :], st[:, b, :])
                        last.then_inc(done, 1)

                    def residual(it, s):
                        dve.wait_ge(x2_in[s], it * 16 + 16)
                        dve.wait_ge(in_pe[s], IN_PE.done(it, "zt"))
                        dve.tensor_tensor(ya[s][:], GT[0], x2b[s][:], ALU.add).then_inc(in_dve[s], 1)
                        norm_stats(it, ya[s], in_s[s], in_mv[s], in_dve[s], IN_DVE)

                    def in_norm(it, s):
                        dve.wait_ge(in_pool[s], IN_POOL.done(it, "rstd"))
                        settle(dve)
                        for b in range(GB):
                            last = dve.tensor_scalar(x3[s][:, b, :], ya[s][:, b, :], in_mv[s][:, b, 0:1],
                                                     in_r[s][:, b:b + 1], ALU.subtract, ALU.mult)
                        last.then_inc(in_dve[s], 1)

                    def k(it, s):
                        dve.wait_ge(qkv_pe[s], QKV_PE.done(it, "k"))
                        dve.tensor_copy(kT[s][:], GT[0]).then_inc(qkv_dve[s], 1)

                    def mask_max(it, s, h):
                        dve.wait_ge(att_pe[s], ATT_PE.done(it, f"sc{h}"))
                        dve.scalar_tensor_tensor(pr[s][h][:], ST[h % 2], SCALE, mask[:].unsqueeze(1).broadcast_to([128, GB, N]),
                                                 ALU.mult, ALU.add).then_inc(att_dve[s], 1)
                        dve.wait_ge(att_dve[s], ATT_DVE.done(it, f"m{h}"))
                        dve.reduce_max(mx[s][:, h, :], pr[s][h][:], AX).then_inc(att_dve[s], 1)

                    def over_sums(it, s):
                        dve.wait_ge(att_pe[s], ATT_PE.done(it, "pv3"))
                        settle(dve)
                        for k in range(2):
                            last = dve.reciprocal(rec[s][:, 2 * k:2 * k + 2, :], OB[k][:, :, :, HD])
                        last.then_inc(out_dve[s], 1)
                        dve.wait_ge(out_dve[s], OUT_DVE.done(it, "rec"))
                        dve.wait_ge(out_pool[s], OUT_POOL.done_before(it, "out"))
                        for k in range(2):
                            last = dve.tensor_tensor(
                                yc[s][:, 2 * k:2 * k + 2, :].rearrange("p b (h e) -> p b h e", h=NH), OB[k][:, :, :, 0:HD],
                                rec[s][:, 2 * k:2 * k + 2, :].unsqueeze(3).broadcast_to([128, 2, NH, HD]), ALU.mult)
                        last.then_inc(out_dve[s], 1)

                    def last_residual(it, s):
                        dve.wait_ge(in_pool[s], IN_POOL.done(it, "keep"))
                        dve.wait_ge(out_dve[s], OUT_DVE.done(it, "att"))
                        dve.tensor_tensor(yc[s][:], yc[s][:], x3k[s][:], ALU.add).then_inc(out_dve[s], 1)
                        norm_stats(it, yc[s], out_s[s], out_mv[s], out_dve[s], OUT_DVE)

                    def slot(it, s, h):
                        each(it, s, 0, mask_max, h)
                        if h == 0:
                            each(it, s, -2, last_residual)
                        if h == 1:
                            each(it, s, 2, residual)
                        if h == 2:
                            each(it, s, -1, over_sums)
                            each(it, s, 1, k)
                        if h == 3:
                            each(it, s, 2, in_norm)

                    over(dve, halves(slot))


def kernel(**inputs):
    import numpy as np
    import concourse.bacc as _bacc
    from concourse.bass_utils import run_bass_kernel_spmd as _run

    a = {k: np.asarray(v) for k, v in inputs.items()}
    l0, l1, l2 = "L0_gnn_", "L1_gnn_", "L2_gnn_"

    def gates_last(b):
        return b.reshape(MAXW, 4, 128).transpose(2, 0, 1).reshape(128, MAXW * 4)

    lay = {
        "x_t": a["x"].transpose(1, 0, 2), "x_f": a["x"].transpose(2, 0, 1),
        "adj": a["adj"], "adjT": a["adj"].T,
        "eb": a[l0 + "edge_bias"], "oeb": a[l0 + "out_edge_bias"],
        "gate_w": np.concatenate([a[l0 + "gate_weight"], a[l0 + "out_gate_weight"], a[l0 + "loop_gate"]], 1),
        "gate_b": np.concatenate([a[l0 + "bias_gate"], a[l0 + "out_bias_gate"]], 1),
        "wg0": a[l1 + "Wg0"], "wg1": a[l1 + "Wg1"], "bg0": a[l1 + "bg0"], "bg1": a[l1 + "bg1"],
        "wihT": a[l1 + "Wih"].transpose(2, 0, 1), "whhT": a[l1 + "Whh"].transpose(2, 0, 1),
        "bih": gates_last(a[l1 + "bih"]), "bhh": gates_last(a[l1 + "bhh"]),
        "w1T": a[l2 + "W1"].T, "w2T": a[l2 + "W2"].T.reshape(H1, 128, D).transpose(1, 0, 2),
        "bn1": np.stack([a[l2 + n].reshape(H1, 128).T for n in ("b1", "g1", "be1")], 1),
        "bn2": np.stack([a[l2 + n] for n in ("b2", "g2", "be2")], 1),
        "w3": a["L3_gnn_W"],
    }
    nc = _bacc.Bacc("TRN2", target_bir_lowering=False, num_devices=1)
    arrays = {f"in_{k}": np.ascontiguousarray(v) for k, v in lay.items()}
    t = {k: nc.dram_tensor(f"in_{k}", arrays[f"in_{k}"].shape, F32, kind="ExternalInput").ap() for k in lay}
    out = nc.dram_tensor("out_dram", (N, B, D), F32, kind="ExternalOutput").ap()
    build(nc, t, out)
    r = _run(nc, [arrays], core_ids=[0])
    return np.ascontiguousarray(r.results[0]["out_dram"].transpose(1, 0, 2))
```

```python
from contextlib import ExitStack

import concourse.bass as bass
from concourse import mybir

F32 = mybir.dt.float32
F32R = mybir.dt.float32r
ALU = mybir.AluOpType
ACT = mybir.ActivationFunctionType
AX = mybir.AxisListType.X

B, N, D = 128, 128, 128
GB = 4
S = 2
NIT = B // (GB * S)
NG = B // GB
C = GB * N
H1 = 2
NH, HD = 4, 32
EPS = 1e-5
MASKED = -3.0e38
MAXW = 4
GI, GF, GG, GO = range(4)


class Steps:

    def __init__(self, *names):
        self.at = {n: k + 1 for k, n in enumerate(names)}
        self.total = len(names)

    def done(self, it, name):
        return it * self.total + (self.total + self.at[name])

    def done_before(self, it, name):
        return it * self.total + self.at[name]


UNITS = [(1, 0, N, 0, GB // 2), (1, 0, N, GB // 2, GB // 2)]
UNITS += [(p, j, N // p, 0, GB) for p in range(2, MAXW + 1) for j in range(p)]
NU = len(UNITS)

PRE_PE = Steps("gates", "in", "out", "ax0", "xw0", "xw1", "ax1")
PRE_DVE = Steps("gates", "in", "out", "acc_in", "acc_out", "y", "stats", "aggr", "x1", "xw0", "xw1", "h_lo")
PRE_ACT = Steps("gates", "loop", "ax0", "h1", "h2")
PRE_POOL = Steps("veps", "rstd")
CELL_PE = Steps(*[f"{u}{x}" for u in range(NU) for x in ("ig", "fo")])
CELL_ACT = Steps(*[f"{u}{x}" for u in range(NU) for x in (("i", "g", "o", "t") if UNITS[u][1] == 0 else ("i", "g", "f", "o", "t"))])
CELL_DVE = Steps(*[f"{u}{x}" for u in range(NU) for x in (("c", "h") if UNITS[u][1] == 0 else ("ig", "fc", "c", "h"))])
POST_PE = Steps("hT", "agg", "w1a", "w1b")
POST_DVE = Steps("y", "stats", "aggr", "x2", "agg_hi", "bna", "bnb")
POST_ACT = Steps("agg")
POST_POOL = Steps("veps", "rstd", "agg_lo")

KEEP = Steps("keep")

MLP_PE = Steps("w1a", "w1b", "w2")
MLP_ACT = Steps("h0", "h1")
MLP_OUT = Steps("out")
MLP_DVE = Steps("hi0", "lo0", "bn")
CUT = Steps("agg")

FILL = {
    0: [("pre", 0, "gates"), ("post", 0, "hT")], 1: [("pre", 0, "sigmoid"), ("pre", 1, "gates"), ("post", 1, "hT")],
    2: [("pre", 1, "sigmoid"), ("pre", 0, "in"), ("post", 0, "stats")], 3: [("pre", 1, "in"), ("post", 1, "stats")],
    4: [("pre", 0, "out"), ("pre", 0, "acc_in"), ("keep", 0, "keep")],
    5: [("pre", 1, "out"), ("pre", 1, "acc_in"), ("keep", 1, "keep")],
    6: [("post", 0, "x2")], 7: [("post", 1, "x2")], 8: [("post", 0, "agg"), ("pre", 0, "y")], 9: [("pre", 1, "y")],
    10: [("post", 1, "agg"), ("pre", 0, "stats")], 11: [("post", 0, "cut"), ("pre", 1, "stats")],
    12: [("post", 1, "cut"), ("pre", 0, "x1")], 13: [("pre", 1, "x1")], 14: [("post", 0, "w1a"), ("pre", 0, "ax0")],
    15: [("post", 1, "w1a"), ("pre", 1, "ax0")], 16: [("pre", 0, "xw0")], 17: [("pre", 0, "h1"), ("pre", 1, "xw0")],
    18: [("post", 0, "w1b"), ("pre", 0, "xw1"), ("pre", 1, "h1")], 19: [("post", 1, "w1b"), ("pre", 1, "xw1")],
    20: [("pre", 0, "ax1")], 21: [("pre", 1, "ax1")],
}
SHIFT = {"pre": 1, "keep": 0, "post": -1}

IN_PE, IN_ACT = Steps("zt"), Steps("z")
IN_DVE, IN_POOL = Steps("y", "stats", "aggr", "x3"), Steps("veps", "rstd")
QKV_PE, QKV_ACT = Steps("x3t", "k", "q", "v"), Steps("x3t", "k", "q", "v")
ATT_PE = Steps("sc0", "sc1", "sc2", "pt0", "sc3", "pt1", "pv0", "pt2", "pv1", "pt3", "pv2", "pv3")
ATT_ACT = Steps("exp0", "exp1", "pt0", "exp2", "pt1", "exp3", "pt2", "pt3")
ATT_DVE = Steps("m0", "max0", "m1", "max1", "m2", "max2", "m3", "max3")
ATT_POOL = Steps("sub0", "sub1", "sub2", "sub3")
SAVE_ACT = Steps("x3k")
OUT_DVE, OUT_POOL, OUT_ACT = Steps("rec", "att", "stats", "aggr"), Steps("y", "veps", "rstd", "mr", "shift"), Steps("out")


def exists(it):
    return not isinstance(it, int) or 0 <= it < NIT


def shift(it, s, n):
    return it + (s + n) // S, (s + n) % S


def each(it, s, n, piece, *args):
    jt, js = shift(it, s, n)
    if exists(jt):
        piece(jt, js, *args)


def over(eng, body, ahead=1, first=None):
    for it in range(-ahead if first is None else first, 1):
        body(it)
    with eng.Fori(1, NIT - ahead) as it:
        body(it)
    for it in range(NIT - ahead, NIT + 1):
        body(it)


def build(nc, t, out):
    x2_dram = nc.dram_tensor("x2_dram", (N, B, D), F32, kind="Internal").ap()

    with ExitStack() as top:
        def sb(name, shape, ctx=top, dtype=F32):
            return ctx.enter_context(nc.sbuf_tensor(name, shape, dtype))

        def parts(name, shape, ctx=top):
            return [sb(f"{name}_{k}", shape, ctx, F32R) for k in ("hi", "lo")]

        def whole(part):
            return part.bitcast(F32)

        def split_matmul(pe, dst, weights, moving, start=True, stop=True):
            (w_hi, w_lo), (m_hi, m_lo) = weights, moving
            pe.matmul(dst, w_hi, m_hi, start=start, stop=False)
            pe.matmul(dst, w_lo, m_hi, start=False, stop=False)
            return pe.matmul(dst, w_hi, m_lo, start=False, stop=stop)

        def sem(name, ctx=top):
            return ctx.enter_context(nc.semaphore(name))

        def flat(ap):
            return ap.rearrange("p a b -> p (a b)")

        bank = [top.enter_context(nc.psum_tensor(f"bank{k}", [128, 512], F32)) for k in range(8)]
        tile = [b[:].rearrange("p (g c) -> p g c", g=GB) for b in bank]

        agg_all = sb("agg_all", [128, B, N])
        ident = sb("ident", [128, 128])
        minus_half = sb("minus_half", [128, GB])
        w1T, w1s = sb("w1T", [128, H1 * 128]), parts("w1s", [128, H1 * 128])
        w2T = sb("w2T", [128, H1, 128])
        w3 = sb("w3", [128, 3 * D])
        mask = sb("mask", [128, 128])
        bn1_stats = sb("bn1_stats", [128, H1, NG, 6])
        bn2_stats = sb("bn2_stats", [128, NG, 6])
        bn1_par = sb("bn1_par", [128, 3, H1])
        bn2_par = sb("bn2_par", [128, 3])
        carrier = sem("carrier")
        adj_in, consts_in, weights_in = sem("adj_in"), sem("consts_in"), sem("weights_in")

        def settle(eng):
            eng.sem_inc(carrier, 1)

        with ExitStack() as one:
            def sb1(name, shape):
                return sb(name, shape, one)

            adj, adjT = sb1("adj", [128, 128]), sb1("adjT", [128, 128])
            w_inT, w_outT = sb1("w_inT", [128, 128]), sb1("w_outT", [128, 128])
            wih1s = parts("wih1s", [128, 512], one)
            a_hatT = sb1("a_hatT", [128, 128])
            eb, oeb = sb1("eb", [128, 128]), sb1("oeb", [128, 128])
            gate_w, gate_b = sb1("gate_w", [128, 3]), sb1("gate_b", [128, 3])
            wg0, wg1 = sb1("wg0", [128, 128]), sb1("wg1", [128, 128])
            bg0, bg1 = sb1("bg0", [128, 128]), sb1("bg1", [128, 128])
            a_bg0 = sb1("a_bg0", [128, 128])
            wihT, whhT = sb1("wihT", [128, MAXW, 512]), sb1("whhT", [128, MAXW, 512])
            bih, bhh, b_cell = (sb1(n, [128, MAXW * 4]) for n in ("bih", "bhh", "b_cell"))
            deg = sb1("deg", [128, 8])

            x_t = [sb1(f"x_t{s}", [128, GB, D]) for s in range(S)]
            x_f = [sb1(f"x_f{s}", [128, GB, N]) for s in range(S)]
            gz, sg = ([sb1(f"{n}{s}", [128, GB, 3]) for s in range(S)] for n in ("gz", "sg"))
            y1 = [sb1(f"y1_{s}", [128, GB, D]) for s in range(S)]
            x1 = [sb1(f"x1_{s}", [128, GB, D]) for s in range(S)]
            x1k = [sb1(f"x1k{s}", [128, GB, D]) for s in range(S)]
            axT, xw, h1T, u_in, u_out = ([sb1(f"{n}{s}", [128, GB, D]) for s in range(S)] for n in ("axT", "xw", "h1T", "u_in", "u_out"))
            hTs, aggs = ([parts(f"{n}{s}", [128, GB, N], one) for s in range(S)] for n in ("hTs", "agg_parts"))
            seq = [sb1(f"seq{s}", [128, GB, N]) for s in range(S)]
            hid = [sb1(f"hid{s}", [128, 256]) for s in range(S)]
            gi, gf, gg, go, ct, cc, ig = ([sb1(f"{n}{s}", [128, 256]) for s in range(S)]
                                          for n in ("gi", "gf", "gg", "go", "ct", "cc", "ig"))
            y2 = [sb1(f"y2_{s}", [128, GB, D]) for s in range(S)]
            x2 = [sb1(f"x2_{s}", [128, GB, D]) for s in range(S)]
            agg = [sb1(f"agg{s}", [128, GB, N]) for s in range(S)]
            ln_s = [sb1(f"ln_s{s}", [128, GB, 6]) for s in range(S)]
            ln_mv = [sb1(f"ln_mv{s}", [128, GB, 2]) for s in range(S)]
            ln_r = [sb1(f"ln_r{s}", [128, GB]) for s in range(S)]
            post_s = [sb1(f"post_s{s}", [128, GB, 6]) for s in range(S)]
            post_mv = [sb1(f"post_mv{s}", [128, GB, 2]) for s in range(S)]
            post_r = [sb1(f"post_r{s}", [128, GB]) for s in range(S)]

            x_in = [sem(f"x_in{s}", one) for s in range(S)]

            def group(it, s):
                return bass.ds(it * (S * GB) + s * GB, GB)

            def load_x(sp, it, s):
                sp.dma_start(x_t[s][:], t["x_t"][:, group(it, s), :]).then_inc(x_in[s], 16)
                sp.dma_start(x_f[s][:], t["x_f"][:, group(it, s), :]).then_inc(x_in[s], 16)

            with ExitStack() as zero:
                pool_set, dve_set, dve_link, pe_set = (sem(n, zero) for n in ("pool_set", "dve_set", "dve_link", "pe_set"))
                tmp, tmp2, origin, an = (sb(n, [128, 128], zero) for n in ("tmp", "tmp2", "origin", "an"))
                with nc.Block() as block:
                    adj_loads = [(adj, t["adj"]), (adjT, t["adjT"])]
                    loads = [(bih, t["bih"]), (bhh, t["bhh"]), (bg0, t["bg0"].partition_broadcast(128)),
                             (eb, t["eb"]), (oeb, t["oeb"]), (wg0, t["wg0"]), (wg1, t["wg1"]),
                             (bg1, t["bg1"].partition_broadcast(128)), (bn1_par, t["bn1"]), (bn2_par, t["bn2"])]
                    CONSTS = 16 * (len(loads) + 2)

                    @block.sync
                    def _(sp):
                        for dst, src in adj_loads:
                            sp.dma_start(dst[:], src).then_inc(adj_in, 16)
                        sp.dma_start(gate_w[:], t["gate_w"]).then_inc(consts_in, 16)
                        sp.dma_start(gate_b[:, 0:2], t["gate_b"]).then_inc(consts_in, 16)
                        for dst, src in loads[:3]:
                            sp.dma_start(dst[:], src).then_inc(consts_in, 16)
                        for s in range(S):
                            load_x(sp, 0, s)
                        for dst, src in loads[3:]:
                            sp.dma_start(dst[:], src).then_inc(consts_in, 16)

                    @block.gpsimd
                    def _(pool):
                        pool.memset(ident[:], 0.0).then_inc(pool_set, 1)
                        pool.memset(minus_half[:], -0.5).then_inc(pool_set, 1)
                        pool.wait_ge(pool_set, 2)
                        pool.affine_select(out=ident[:], in_=ident[:], compare_op=ALU.not_equal, fill=1.0, base=0,
                                           pattern=[[-1, 128]], channel_multiplier=1).then_inc(pool_set, 1)
                        pool.memset(gate_b[:, 2:3], 0.0).then_inc(pool_set, 1)
                        pool.wait_ge(dve_set, 11)
                        pool.tensor_tensor(deg[:, 4:5], deg[:, 3:4], minus_half[:, 0:1], ALU.pow).then_inc(pool_set, 1)

                    @block.vector
                    def _(dve):
                        done = [0]

                        def step(ins):
                            done[0] += 1
                            ins.then_inc(dve_set, 1)
                            dve.wait_ge(dve_set, done[0])

                        dve.wait_ge(adj_in, 16 * len(adj_loads))
                        dve.wait_ge(pool_set, 3)
                        step(nc.vector.tensor_scalar(tmp[:], adjT[:], 0.0, None, ALU.is_gt))
                        step(nc.vector.scalar_tensor_tensor(tmp2[:], adjT[:], 0.0, tmp[:], ALU.min, ALU.add))
                        step(nc.vector.tensor_tensor(w_inT[:], tmp2[:], adjT[:], ALU.mult))
                        step(nc.vector.tensor_scalar(tmp[:], adj[:], 0.0, None, ALU.is_gt))
                        step(nc.vector.scalar_tensor_tensor(origin[:], adj[:], 0.0, tmp[:], ALU.min, ALU.add))
                        step(nc.vector.tensor_tensor(w_outT[:], origin[:], adjT[:], ALU.mult))
                        step(nc.vector.tensor_tensor(an[:], adj[:], ident[:], ALU.add))
                        step(nc.vector.reduce_sum(deg[:, 0:1], an[:], AX))
                        step(nc.vector.tensor_tensor(tmp[:], adjT[:], ident[:], ALU.add))
                        step(nc.vector.tensor_tensor(tmp2[:], ident[:], an[:], ALU.mult))
                        nc.vector.reduce_sum(deg[:, 1:2], tmp[:], AX)
                        nc.vector.reduce_sum(deg[:, 2:3], tmp2[:], AX).then_inc(dve_link, 1)
                        dve.wait_ge(dve_link, 1)
                        nc.vector.tensor_tensor(deg[:, 5:6], deg[:, 1:2], deg[:, 2:3], ALU.subtract).then_inc(dve_link, 1)
                        dve.wait_ge(dve_link, 2)
                        step(nc.vector.tensor_tensor(deg[:, 3:4], deg[:, 0:1], deg[:, 5:6], ALU.add))
                        step(nc.vector.tensor_scalar(mask[:], adj[:], 0.0, MASKED, ALU.is_equal, ALU.mult))
                        dve.wait_ge(consts_in, CONSTS)
                        step(nc.vector.tensor_tensor(b_cell[:], bih[:], bhh[:], ALU.add))
                        dve.wait_ge(pool_set, 5)
                        step(nc.vector.tensor_scalar(tmp[:], ident[:], deg[:, 4:5], None, ALU.mult))
                        dve.wait_ge(pe_set, 1)
                        step(nc.vector.tensor_scalar(a_hatT[:], bank[0][:, 0:128], deg[:, 4:5], None, ALU.mult))
                        dve.wait_ge(pe_set, 2)
                        step(nc.vector.tensor_copy(a_bg0[:], bank[1][:, 0:128]))

                    @block.tensor
                    def _(pe):
                        pe.wait_ge(dve_set, 14)
                        pe.matmul(bank[0][:, 0:128], an[:], tmp[:], start=True, stop=True).then_inc(pe_set, 1)
                        pe.wait_ge(consts_in, CONSTS)
                        pe.matmul(bank[1][:, 0:128], bg0[:], adjT[:], start=True, stop=True).then_inc(pe_set, 1)

            split_set = sem("split_set", one)
            x2_out = [sem(f"x2_out{s}", one) for s in range(S)]
            agg_out = [sem(f"agg_out{s}", one) for s in range(S)]
            pre_pe, pre_act, pre_dve, pre_pool, keep_pool, cell_pe, cell_act, cell_dve, post_pe, post_act, post_dve, post_pool = (
                [sem(f"{n}{s}", one) for s in range(S)]
                for n in ("pre_pe", "pre_act", "pre_dve", "pre_pool", "keep_pool", "cell_pe", "cell_act", "cell_dve",
                          "post_pe", "post_act", "post_dve", "post_pool"))
            PB = [bank[0], bank[1]]
            QB = [bank[2], bank[3]]
            PT, QT = [tile[0], tile[1]], [tile[2], tile[3]]
            GATE = [[bank[4], bank[5]], [bank[6], bank[7]]]

            weight_loads = [(wihT, t["wihT"]), (whhT, t["whhT"]), (w1T, t["w1T"]), (w2T, t["w2T"]), (w3, t["w3"])]

            def body_of(unit, piece):
                def body(it):
                    def fill(k):
                        for stage, s, name in FILL.get(k, []):
                            if exists(it + SHIFT[stage]):
                                piece(stage, it + SHIFT[stage], s, name)
                    for u in range(NU):
                        for s in range(S):
                            k = S * u + s
                            if exists(it):
                                unit(it, s, u, lambda k=k: fill(k))
                            else:
                                fill(k)
                return body

            with nc.Block() as block:
                @block.sync
                def _(sp):
                    for s in range(S):
                        sp.sem_inc(x2_out[s], 16)
                        sp.sem_inc(agg_out[s], 16)

                    def body(it):
                        if exists(it - 1):
                            for s in range(S):
                                sp.wait_ge(post_dve[s], POST_DVE.done(it - 1, "x2"))
                                settle(sp)
                                sp.dma_start(x2_dram[:, group(it - 1, s), :], x2[s][:]).then_inc(x2_out[s], 16)
                                sp.wait_ge(post_act[s], POST_ACT.done(it - 1, "agg"))
                                settle(sp)
                                sp.dma_start(agg_all[:, group(it - 1, s), :], agg[s][:]).then_inc(agg_out[s], 16)
                        if exists(it + 2):
                            for s in range(S):
                                sp.wait_ge(pre_dve[s], PRE_DVE.done_before(it + 2, "y"))
                                settle(sp)
                                sp.wait_ge(pre_pe[s], PRE_PE.done_before(it + 2, "gates"))
                                settle(sp)
                                load_x(sp, it + 2, s)

                    for dst, src in weight_loads:
                        sp.dma_start(dst[:], src).then_inc(weights_in, 16)
                    for it in (-1, 0):
                        body(it)
                    with sp.Fori(1, NIT - 2) as it:
                        body(it)
                    for it in (NIT - 2, NIT - 1, NIT):
                        body(it)
                    for s in range(S):
                        sp.wait_ge(agg_out[s], 16 * NIT + 16)
                        sp.wait_ge(x2_out[s], 16 * NIT + 16)

                @block.tensor
                def _(pe):
                    for s in range(S):
                        pe.sem_inc(pre_pe[s], PRE_PE.total)
                        pe.sem_inc(cell_pe[s], CELL_PE.total)
                        pe.sem_inc(post_pe[s], POST_PE.total)

                    def per_graph(dst, stationary, moving, transpose=False):
                        for b in range(GB):
                            if transpose:
                                last = pe.transpose(dst[:, b, :], stationary[:, b, :], ident[:])
                            else:
                                last = pe.matmul(dst[:, b, :], stationary[:, b, :], moving, start=True, stop=True)
                        return last

                    def pre(it, s, name):
                        if name == "gates":
                            pe.wait_ge(pre_dve[s], PRE_DVE.done_before(it, "h_lo"))
                            pe.wait_ge(x_in[s], it * 32 + 32)
                            for b in range(GB):
                                last = pe.matmul(PB[s][:, 3 * b:3 * b + 3], x_f[s][:, b, :], gate_w[:], start=True, stop=True)
                            last.then_inc(pre_pe[s], 1)
                        elif name == "in":
                            pe.wait_ge(pre_dve[s], PRE_DVE.done(it, "gates"))
                            pe.matmul(PB[s][:], w_inT[:], flat(x_t[s][:]), start=True, stop=True).then_inc(pre_pe[s], 1)
                        elif name == "out":
                            pe.wait_ge(pre_dve[s], PRE_DVE.done(it, "in"))
                            pe.matmul(PB[s][:], w_outT[:], flat(x_t[s][:]), start=True, stop=True).then_inc(pre_pe[s], 1)
                        elif name == "ax0":
                            pe.wait_ge(pre_dve[s], PRE_DVE.done(it, "x1"))
                            per_graph(PT[s], x1[s], adjT[:]).then_inc(pre_pe[s], 1)
                        elif name == "xw0":
                            pe.wait_ge(pre_act[s], PRE_ACT.done(it, "ax0"))
                            pe.matmul(PB[s][:], wg0[:], flat(axT[s][:]), start=True, stop=True).then_inc(pre_pe[s], 1)
                        elif name == "xw1":
                            pe.wait_ge(pre_act[s], PRE_ACT.done(it, "h1"))
                            per_graph(PT[s], h1T[s], wg1[:]).then_inc(pre_pe[s], 1)
                        elif name == "ax1":
                            pe.wait_ge(pre_dve[s], PRE_DVE.done(it, "xw1"))
                            per_graph(PT[s], xw[s], adjT[:]).then_inc(pre_pe[s], 1)

                    def cell(it, s, u, inside):
                        p, j, nw, b0, nb = UNITS[u]
                        n = nw * nb
                        if j == 0:
                            inside()
                        seen = seq[s][:, :, bass.ds(j, nw, p)]
                        slot = {GI: GATE[s][0][:, 0:n], GG: GATE[s][0][:, 256:256 + n],
                                GF: GATE[s][1][:, 0:n], GO: GATE[s][1][:, 256:256 + n]}

                        def out3(g):
                            return slot[g].rearrange("p (b w) -> p b w", b=nb)

                        def wx(g):
                            return wihT[:, p - 1, g * 128:(g + 1) * 128]

                        def wh(g):
                            return whhT[:, p - 1, g * 128:(g + 1) * 128]

                        if u == 0:
                            pe.wait_ge(pre_dve[s], PRE_DVE.done(it, "h_lo"))
                            pe.wait_ge(cell_act[s], CELL_ACT.done_before(it, f"{NU - 1}o"))
                        elif j or p == 1:
                            pe.wait_ge(cell_act[s], CELL_ACT.done(it, f"{u - 1}o"))
                        else:
                            pe.wait_ge(cell_dve[s], CELL_DVE.done(it, f"{u - 1}h"))
                        if j == 0:
                            def from_x(g):
                                if p == 1:
                                    return split_matmul(pe, slot[g], [w[:, g * 128:(g + 1) * 128] for w in wih1s],
                                                        [flat(h[:, b0:b0 + nb, :]) for h in hTs[s]])
                                return pe.matmul(out3(g), wx(g), seen, start=True, stop=True)

                            from_x(GI)
                            from_x(GG).then_inc(cell_pe[s], 1)
                            from_x(GO).then_inc(cell_pe[s], 1)
                            return
                        hs = hid[s][:, 0:n]
                        for k, g in enumerate((GI, GG, GF, GO)):
                            pe.matmul(out3(g), wx(g), seen, start=(k % 2 == 0), stop=False, skip_group_check=True)
                        inside()
                        pe.wait_ge(cell_dve[s], CELL_DVE.done(it, f"{u - 1}h"))
                        for k, g in enumerate((GI, GG, GF, GO)):
                            last = pe.matmul(slot[g], wh(g), hs, start=False, stop=True, skip_group_check=True)
                            if k % 2:
                                last.then_inc(cell_pe[s], 1)

                    def post(it, s, name):
                        if name == "hT":
                            pe.wait_ge(cell_dve[s], CELL_DVE.done(it, f"{NU - 1}h"))
                            pe.wait_ge(post_dve[s], POST_DVE.done_before(it, "bnb"))
                            per_graph(QT[s], seq[s], None, True).then_inc(post_pe[s], 1)
                        elif name == "agg":
                            pe.wait_ge(post_dve[s], POST_DVE.done(it, "x2"))
                            per_graph(QT[s], x2[s], a_hatT[:]).then_inc(post_pe[s], 1)
                        elif name == "w1a":
                            pe.wait_ge(post_act[s], POST_ACT.done(it, "agg"))
                            pe.wait_ge(post_pool[s], POST_POOL.done(it, "agg_lo"))
                            split_matmul(pe, QB[s][:], [w[:, 0:128] for w in w1s], [flat(a[:]) for a in aggs[s]]).then_inc(post_pe[s], 1)
                        elif name == "w1b":
                            pe.wait_ge(post_dve[s], POST_DVE.done(it, "bna"))
                            split_matmul(pe, QB[s][:], [w[:, 128:256] for w in w1s], [flat(a[:]) for a in aggs[s]]).then_inc(post_pe[s], 1)

                    def piece(stage, it, s, name):
                        if stage != "keep":
                            (pre if stage == "pre" else post)(it, s, name)

                    body = body_of(cell, piece)
                    body(-1)
                    pe.wait_ge(weights_in, 16 * len(weight_loads))
                    pe.wait_ge(split_set, 4)
                    over(pe, body, first=0)

                @block.scalar
                def _(act):
                    for s in range(S):
                        act.sem_inc(pre_act[s], PRE_ACT.total)
                        act.sem_inc(cell_act[s], CELL_ACT.total)
                        act.sem_inc(post_act[s], POST_ACT.total)

                    def piece(stage, it, s, name):
                        if name == "sigmoid":
                            act.wait_ge(pre_dve[s], PRE_DVE.done(it, "gates"))
                            act.activation(sg[s][:], gz[s][:], ACT.Sigmoid).then_inc(pre_act[s], 1)
                        elif name == "in":
                            act.wait_ge(pre_act[s], PRE_ACT.done(it, "gates"))
                            for b in range(GB):
                                last = act.activation(y1[s][:, b, :], x_t[s][:, b, :], ACT.Copy, scale=sg[s][:, b, 2:3])
                            last.then_inc(pre_act[s], 1)
                        elif name == "ax0":
                            act.wait_ge(pre_pe[s], PRE_PE.done(it, "ax0"))
                            act.activation(axT[s][:], PT[s], ACT.Copy).then_inc(pre_act[s], 1)
                        elif name == "h1":
                            act.wait_ge(pre_dve[s], PRE_DVE.done(it, "xw0"))
                            act.activation(h1T[s][:], xw[s][:], ACT.Relu).then_inc(pre_act[s], 1)
                        elif name == "ax1":
                            act.wait_ge(pre_pe[s], PRE_PE.done(it, "ax1"))
                            act.activation(hTs[s][0][:], PT[s], ACT.Relu).then_inc(pre_act[s], 1)
                        elif name == "agg":
                            act.wait_ge(agg_out[s], it * 16 + 16)
                            act.wait_ge(post_pe[s], POST_PE.done(it, "agg"))
                            act.activation(agg[s][:], QT[s], ACT.Copy).then_inc(post_act[s], 1)

                    def cell(it, s, u, inside):
                        p, j, nw, b0, nb = UNITS[u]
                        n = nw * nb

                        def gate(dst, g, func):
                            k, at = {GI: (0, 0), GG: (0, 256), GF: (1, 0), GO: (1, 256)}[g]
                            col = 4 * (p - 1) + g
                            act.activation(dst[s][:, 0:n], GATE[s][k][:, at:at + n], func,
                                           bias=b_cell[:, col:col + 1]).then_inc(cell_act[s], 1)

                        act.wait_ge(cell_pe[s], CELL_PE.done(it, f"{u}ig"))
                        gate(gi, GI, ACT.Sigmoid)
                        gate(gg, GG, ACT.Tanh)
                        act.wait_ge(cell_pe[s], CELL_PE.done(it, f"{u}fo"))
                        if j:
                            gate(gf, GF, ACT.Sigmoid)
                        if u == 1:
                            act.wait_ge(cell_dve[s], CELL_DVE.done(it, "0h"))
                        if u == 0:
                            act.wait_ge(cell_dve[s], CELL_DVE.done_before(it, f"{NU - 1}h"))
                        gate(go, GO, ACT.Sigmoid)
                        inside()
                        act.wait_ge(cell_dve[s], CELL_DVE.done(it, f"{u}c"))
                        act.activation(ct[s][:, 0:n], cc[s][:, 0:n], ACT.Tanh).then_inc(cell_act[s], 1)

                    over(act, body_of(cell, piece))

                @block.vector
                def _(dve):
                    for s in range(S):
                        dve.sem_inc(pre_dve[s], PRE_DVE.total)
                        dve.sem_inc(cell_dve[s], CELL_DVE.total)
                        dve.sem_inc(post_dve[s], POST_DVE.total)

                    def pre(it, s, name):
                        def own(step):
                            dve.wait_ge(pre_dve[s], PRE_DVE.done(it, step))

                        def wide(m):
                            return m[:].unsqueeze(1).broadcast_to([128, GB, m.shape[-1]])

                        if name == "gates":
                            dve.wait_ge(pre_pe[s], PRE_PE.done(it, "gates"))
                            dve.tensor_tensor(gz[s][:], PB[s][:, 0:3 * GB].rearrange("p (b g) -> p b g", g=3), wide(gate_b),
                                              ALU.add).then_inc(pre_dve[s], 1)
                        elif name == "in":
                            dve.wait_ge(pre_pe[s], PRE_PE.done(it, "in"))
                            dve.tensor_tensor(u_in[s][:], PT[s], wide(eb), ALU.add).then_inc(pre_dve[s], 1)
                        elif name == "out":
                            dve.wait_ge(pre_pe[s], PRE_PE.done(it, "out"))
                            dve.tensor_tensor(u_out[s][:], PT[s], wide(oeb), ALU.add).then_inc(pre_dve[s], 1)
                        elif name == "acc_in":
                            own("in")
                            dve.wait_ge(pre_act[s], PRE_ACT.done(it, "loop"))
                            for b in range(GB):
                                last = dve.scalar_tensor_tensor(y1[s][:, b, :], u_in[s][:, b, :], sg[s][:, b, 0:1],
                                                                y1[s][:, b, :], ALU.mult, ALU.add)
                            last.then_inc(pre_dve[s], 1)
                        elif name == "y":
                            own("acc_in")
                            for b in range(GB):
                                last = dve.scalar_tensor_tensor(y1[s][:, b, :], u_out[s][:, b, :], sg[s][:, b, 1:2],
                                                                y1[s][:, b, :], ALU.mult, ALU.add)
                            last.then_inc(pre_dve[s], 1)
                            own("acc_out")
                            dve.scalar_tensor_tensor(y1[s][:], y1[s][:], 0.0, x_t[s][:], ALU.max, ALU.add).then_inc(pre_dve[s], 1)
                        elif name == "stats":
                            own("y")
                            settle(dve)
                            for b in range(GB):
                                last = dve.bn_stats(ln_s[s][:, b, :], y1[s][:, b, :])
                            last.then_inc(pre_dve[s], 1)
                            own("stats")
                            settle(dve)
                            for b in range(GB):
                                last = dve.bn_aggr(ln_mv[s][:, b, :], ln_s[s][:, b, :])
                            last.then_inc(pre_dve[s], 1)
                        elif name == "x1":
                            dve.wait_ge(keep_pool[s], KEEP.done_before(it, "keep"))
                            dve.wait_ge(pre_pool[s], PRE_POOL.done(it, "rstd"))
                            settle(dve)
                            for b in range(GB):
                                last = dve.tensor_scalar(x1[s][:, b, :], y1[s][:, b, :], ln_mv[s][:, b, 0:1],
                                                         ln_r[s][:, b:b + 1], ALU.subtract, ALU.mult)
                            last.then_inc(pre_dve[s], 1)
                        elif name == "ax1":
                            dve.wait_ge(pre_act[s], PRE_ACT.done(it, "h2"))
                            dve.scalar_tensor_tensor(hTs[s][1][:], PT[s], 0.0, whole(hTs[s][0][:]), ALU.max,
                                                     ALU.subtract).then_inc(pre_dve[s], 1)
                        elif name in ("xw0", "xw1"):
                            dve.wait_ge(pre_pe[s], PRE_PE.done(it, name))
                            dve.tensor_tensor(xw[s][:], PT[s], wide(a_bg0 if name == "xw0" else bg1), ALU.add).then_inc(pre_dve[s], 1)

                    def cell(it, s, u, inside):
                        p, j, nw, b0, nb = UNITS[u]
                        n = nw * nb
                        a, b, c, d = (x[s][:, 0:n] for x in (gi, gg, cc, ig))
                        dve.wait_ge(cell_act[s], CELL_ACT.done(it, f"{u}g"))
                        dve.tensor_tensor(c if j == 0 else d, a, b, ALU.mult).then_inc(cell_dve[s], 1)
                        if j:
                            dve.wait_ge(cell_act[s], CELL_ACT.done(it, f"{u}f"))
                            dve.tensor_tensor(c, gf[s][:, 0:n], c, ALU.mult).then_inc(cell_dve[s], 1)
                            dve.wait_ge(cell_dve[s], CELL_DVE.done(it, f"{u}fc"))
                            dve.tensor_tensor(c, c, d, ALU.add).then_inc(cell_dve[s], 1)
                        inside()
                        if u == 0:
                            dve.wait_ge(post_pe[s], POST_PE.done_before(it, "hT"))
                        dve.wait_ge(cell_act[s], CELL_ACT.done(it, f"{u}t"))
                        if j == p - 1:
                            o = seq[s][:, b0:b0 + nb, bass.ds(j, nw, p)] if p > 1 else seq[s][:, b0:b0 + nb, :]
                        else:
                            o = hid[s][:, 0:n].rearrange("p (b w) -> p b w", b=nb)
                        dve.tensor_tensor(o, go[s][:, 0:n].rearrange("p (b w) -> p b w", b=nb),
                                          ct[s][:, 0:n].rearrange("p (b w) -> p b w", b=nb), ALU.mult).then_inc(cell_dve[s], 1)

                    def post(it, s, name):
                        def own(step):
                            dve.wait_ge(post_dve[s], POST_DVE.done(it, step))
                            settle(dve)

                        if name == "hT":
                            dve.wait_ge(keep_pool[s], KEEP.done(it, "keep"))
                            dve.wait_ge(post_pe[s], POST_PE.done(it, "hT"))
                            dve.tensor_tensor(y2[s][:], QT[s], x1k[s][:], ALU.add).then_inc(post_dve[s], 1)
                        elif name == "stats":
                            own("y")
                            for b in range(GB):
                                last = dve.bn_stats(post_s[s][:, b, :], y2[s][:, b, :])
                            last.then_inc(post_dve[s], 1)
                            own("stats")
                            for b in range(GB):
                                last = dve.bn_aggr(post_mv[s][:, b, :], post_s[s][:, b, :])
                            last.then_inc(post_dve[s], 1)
                        elif name == "x2":
                            dve.wait_ge(x2_out[s], it * 16 + 16)
                            dve.wait_ge(post_pool[s], POST_POOL.done(it, "rstd"))
                            settle(dve)
                            for b in range(GB):
                                last = dve.tensor_scalar(x2[s][:, b, :], y2[s][:, b, :], post_mv[s][:, b, 0:1],
                                                         post_r[s][:, b:b + 1], ALU.subtract, ALU.mult)
                            last.then_inc(post_dve[s], 1)
                        elif name == "cut":
                            dve.wait_ge(post_act[s], POST_ACT.done(it, "agg"))
                            settle(dve)
                            dve.tensor_copy(aggs[s][0][:], agg[s][:]).then_inc(post_dve[s], 1)
                        elif name in ("w1a", "w1b"):
                            dve.wait_ge(post_pe[s], POST_PE.done(it, name))
                            settle(dve)
                            stats = bn1_stats[:, int(name == "w1b"), bass.ds(it * S + s, 1), :]
                            dve.bn_stats(stats.rearrange("p a b -> p (a b)"), QB[s][:]).then_inc(post_dve[s], 1)

                    def piece(stage, it, s, name):
                        if stage != "keep":
                            (pre if stage == "pre" else post)(it, s, name)

                    over(dve, body_of(cell, piece))

                @block.gpsimd
                def _(pool):
                    for s in range(S):
                        pool.sem_inc(pre_pool[s], PRE_POOL.total)
                        pool.sem_inc(keep_pool[s], KEEP.total)
                        pool.sem_inc(post_pool[s], POST_POOL.total)

                    def rstd(r, mv, done, steps, it):
                        settle(pool)
                        pool.tensor_scalar(r[:], mv[:, :, 1], EPS, None, ALU.add).then_inc(done, 1)
                        pool.wait_ge(done, steps.done(it, "veps"))
                        pool.tensor_tensor(r[:], r[:], minus_half[:], ALU.pow).then_inc(done, 1)

                    def piece(stage, it, s, name):
                        if name == "cut":
                            pool.wait_ge(post_dve[s], POST_DVE.done(it, "agg_hi"))
                            pool.tensor_tensor(aggs[s][1][:], agg[s][:], whole(aggs[s][0][:]), ALU.subtract).then_inc(post_pool[s], 1)
                        elif stage == "pre" and name == "stats":
                            pool.wait_ge(pre_dve[s], PRE_DVE.done(it, "aggr"))
                            rstd(ln_r[s], ln_mv[s], pre_pool[s], PRE_POOL, it)
                        elif name == "stats":
                            pool.wait_ge(post_dve[s], POST_DVE.done(it, "aggr"))
                            rstd(post_r[s], post_mv[s], post_pool[s], POST_POOL, it)
                        elif name == "keep":
                            pool.wait_ge(post_dve[s], POST_DVE.done_before(it, "y"))
                            settle(pool)
                            pool.wait_ge(pre_dve[s], PRE_DVE.done(it, "x1"))
                            settle(pool)
                            pool.tensor_copy(x1k[s][:], x1[s][:]).then_inc(keep_pool[s], 1)

                    body = body_of(lambda it, s, u, inside: inside(), piece)
                    body(-1)
                    pool.wait_ge(weights_in, 16 * len(weight_loads))
                    for k, (w, (hi, lo)) in enumerate(((wihT[:, 0, :], wih1s), (w1T[:], w1s))):
                        pool.tensor_copy(hi[:], w).then_inc(split_set, 1)
                        pool.wait_ge(split_set, 2 * k + 1)
                        pool.tensor_tensor(lo[:], w, whole(hi[:]), ALU.subtract).then_inc(split_set, 1)
                    over(pool, body, first=0)

        bn1_mv = sb("bn1_mv", [128, H1, 2])
        bn1_scale, bn1_shift = sb("bn1_scale", [128, H1]), sb("bn1_shift", [128, H1])
        bn2_mv = sb("bn2_mv", [128, 2])
        bn2_scale, bn2_shift = sb("bn2_scale", [128, 1]), sb("bn2_shift", [128, 1])
        bn_tmp = sb("bn_tmp", [128, 2 * H1])

        def bn_dve(dve, s_dve, s_pool, n, stats, mv, b, g, be, scale, shift):
            count = [0]

            def step(ins):
                ins.then_inc(s_dve, 1)
                count[0] += 1
                dve.wait_ge(s_dve, count[0])
            for k in range(n):
                step(dve.bn_aggr(mv[k], stats[k]))
            mean_ap = bn_mean(mv, n)
            step(dve.tensor_tensor(bn_tmp[:, 0:n], mean_ap, b, ALU.add))
            step(dve.tensor_tensor(bn_tmp[:, n:2 * n], b, bn_tmp[:, 0:n], ALU.subtract))
            dve.wait_ge(s_pool, 2)
            step(dve.tensor_tensor(scale, scale, g, ALU.mult))
            step(dve.tensor_tensor(bn_tmp[:, 0:n], bn_tmp[:, n:2 * n], scale, ALU.mult))
            step(dve.tensor_tensor(shift, bn_tmp[:, 0:n], be, ALU.add))
            return count[0]

        def bn_mean(mv, n):
            return bn1_mv[:, :, 0] if n == H1 else bn2_mv[:, 0:1]

        def bn_pool(pool, s_dve, s_pool, n, var, scale):
            pool.wait_ge(s_dve, n)
            pool.tensor_scalar(scale, var, EPS, None, ALU.add).then_inc(s_pool, 1)
            pool.wait_ge(s_pool, 1)
            pool.tensor_tensor(scale, scale, minus_half[:, 0:n], ALU.pow).then_inc(s_pool, 1)

        with ExitStack() as two:
            bn1_dve, bn1_pool = sem("bn1_dve", two), sem("bn1_pool", two)
            w_hi_done, w_lo_done = sem("w_hi_done", two), sem("w_lo_done", two)
            mlp_pe, mlp_act, mlp_dve, mlp_out, cut_dve, cut_pool = (
                [sem(f"{n}{s}", two) for s in range(S)]
                for n in ("mlp_pe", "mlp_act", "mlp_dve", "mlp_out", "cut_dve", "cut_pool"))
            w2s = parts("w2s", [128, 128], two)
            aggs = [parts(f"aggs{s}", [128, GB, N], two) for s in range(S)]
            hid1 = [sb(f"hid1_{s}", [128, H1, C], two) for s in range(S)]
            hids = [parts(f"hids{s}", [128, C], two) for s in range(S)]
            BN1_DONE = H1 + 5
            W1B = [[bank[0], bank[1]], [bank[2], bank[3]]]
            W2B = [bank[4], bank[5]]

            def cols(it, s):
                return agg_all[:, bass.ds(it * (S * GB) + s * GB, GB), :]

            def groups(group):
                def body(it):
                    for s in range(S):
                        group(it, s)
                return body

            with nc.Block() as block:
                @block.gpsimd
                def _(pool):
                    for s in range(S):
                        pool.sem_inc(cut_pool[s], CUT.total)
                    pool.wait_ge(w_hi_done, 1)
                    pool.tensor_tensor(w2s[1][:], w2T[:, 0, :], whole(w2s[0][:]), ALU.subtract).then_inc(w_lo_done, 1)

                    def agg_lo(it, s):
                        pool.wait_ge(cut_dve[s], CUT.done(it, "agg"))
                        settle(pool)
                        pool.tensor_tensor(aggs[s][1][:], cols(it, s), whole(aggs[s][0][:]), ALU.subtract).then_inc(cut_pool[s], 1)

                    def group(it, s):
                        each(it, s, 2, agg_lo)

                    body = groups(group)
                    body(-1)
                    bn_pool(pool, bn1_dve, bn1_pool, H1, bn1_mv[:, :, 1], bn1_scale[:])
                    over(pool, body, first=0)

                @block.tensor
                def _(pe):
                    for s in range(S):
                        pe.sem_inc(mlp_pe[s], MLP_PE.total)
                    pe.wait_ge(w_lo_done, 1)

                    def first(it, s):
                        for h in range(H1):
                            pe.wait_ge(mlp_act[s], MLP_ACT.done_before(it, f"h{h}"))
                            pe.wait_ge(cut_pool[s], CUT.done(it, "agg"))
                            split_matmul(pe, W1B[s][h][:], [w[:, h * 128:(h + 1) * 128] for w in w1s],
                                         [flat(a[:]) for a in aggs[s]]).then_inc(mlp_pe[s], 1)

                    def second(it, s):
                        pe.wait_ge(mlp_out[s], MLP_OUT.done_before(it, "out"))
                        pe.wait_ge(mlp_dve[s], MLP_DVE.done_before(it, "bn"))
                        pe.wait_ge(mlp_dve[s], MLP_DVE.done(it, "lo0"))
                        split_matmul(pe, W2B[s][:], [w[:] for w in w2s], [h[:] for h in hids[s]], stop=False)
                        pe.wait_ge(mlp_act[s], MLP_ACT.done(it, "h1"))
                        pe.matmul(W2B[s][:], w2T[:, 1, :], hid1[s][:, 1, :], start=False, stop=True).then_inc(mlp_pe[s], 1)

                    def group(it, s):
                        each(it, s, -1, second)
                        each(it, s, 1, first)

                    over(pe, groups(group))

                @block.scalar
                def _(act):
                    for s in range(S):
                        act.sem_inc(mlp_act[s], MLP_ACT.total)
                        act.sem_inc(mlp_out[s], MLP_OUT.total)
                    act.activation(w2s[0][:], w2T[:, 0, :], ACT.Copy).then_inc(w_hi_done, 1)
                    act.wait_ge(bn1_dve, BN1_DONE)

                    def hidden(it, s):
                        for h, name in enumerate(("w1a", "w1b")):
                            if h:
                                act.wait_ge(mlp_pe[s], MLP_PE.done_before(it, "w2"))
                            else:
                                act.wait_ge(mlp_dve[s], MLP_DVE.done_before(it, "lo0"))
                            settle(act)
                            act.wait_ge(mlp_pe[s], MLP_PE.done(it, name))
                            act.activation(hid1[s][:, h, :], W1B[s][h][:], ACT.Relu, bias=bn1_shift[:, h:h + 1],
                                           scale=bn1_scale[:, h:h + 1]).then_inc(mlp_act[s], 1)

                    def output(it, s):
                        act.wait_ge(mlp_dve[s], MLP_DVE.done(it, "bn"))
                        settle(act)
                        act.activation(cols(it, s), W2B[s][:].rearrange("p (b n) -> p b n", b=GB),
                                       ACT.Copy).then_inc(mlp_out[s], 1)

                    def group(it, s):
                        each(it, s, 0, hidden)
                        each(it, s, -2, output)

                    over(act, groups(group))

                @block.vector
                def _(dve):
                    for s in range(S):
                        dve.sem_inc(mlp_dve[s], MLP_DVE.total)
                        dve.sem_inc(cut_dve[s], CUT.total)

                    def agg_hi(it, s):
                        dve.wait_ge(mlp_pe[s], MLP_PE.done_before(it, "w1b"))
                        settle(dve)
                        dve.tensor_copy(aggs[s][0][:], cols(it, s)).then_inc(cut_dve[s], 1)

                    def half0(it, s):
                        dve.wait_ge(mlp_act[s], MLP_ACT.done(it, "h0"))
                        dve.wait_ge(mlp_pe[s], MLP_PE.done_before(it, "w2"))
                        dve.tensor_copy(hids[s][0][:], hid1[s][:, 0, :]).then_inc(mlp_dve[s], 1)
                        dve.wait_ge(mlp_dve[s], MLP_DVE.done(it, "hi0"))
                        dve.tensor_tensor(hids[s][1][:], hid1[s][:, 0, :], whole(hids[s][0][:]),
                                          ALU.subtract).then_inc(mlp_dve[s], 1)

                    def stats(it, s):
                        dve.wait_ge(mlp_pe[s], MLP_PE.done(it, "w2"))
                        settle(dve)
                        dve.bn_stats(bn2_stats[:, bass.ds(it * S + s, 1), :].rearrange("p a b -> p (a b)"),
                                     W2B[s][:]).then_inc(mlp_dve[s], 1)

                    def group(it, s):
                        each(it, s, -2, stats)
                        each(it, s, 2, agg_hi)
                        each(it, s, 0, half0)

                    body = groups(group)
                    body(-1)
                    n = bn_dve(dve, bn1_dve, bn1_pool, H1, [bn1_stats[:, h, :, :].rearrange("p a b -> p (a b)") for h in range(H1)],
                               [bn1_mv[:, h, :] for h in range(H1)], bn1_par[:, 0, :], bn1_par[:, 1, :], bn1_par[:, 2, :],
                               bn1_scale[:], bn1_shift[:])
                    assert n == BN1_DONE
                    over(dve, body, first=0)

        with ExitStack() as three:
            def sb3(name, shape):
                return sb(name, shape, three)

            bn2_dve, bn2_pool = sem("bn2_dve", three), sem("bn2_pool", three)
            fixed_set = sem("fixed_set", three)
            x2_in, out_done = ([sem(f"{n}{s}", three) for s in range(S)] for n in ("x2_in", "out_done"))
            in_pe, in_act, in_dve, in_pool, qkv_pe, qkv_act, att_pe, att_act, att_dve, att_pool, save_act, out_dve, out_pool, out_act = (
                [sem(f"{n}{s}", three) for s in range(S)]
                for n in ("in_pe", "in_act", "in_dve", "in_pool", "qkv_pe", "qkv_act", "att_pe", "att_act", "att_dve",
                          "att_pool", "save_act", "out_dve", "out_pool", "out_act"))
            x2b = [sb3(f"x2b{s}", [128, GB, D]) for s in range(S)]
            z, ya, yc, x3, x3k, x3T, qT, fin = ([sb3(f"{n}{s}", [128, GB, D]) for s in range(S)]
                                                    for n in ("z", "ya", "yc", "x3_", "x3k", "x3T", "qT", "fin"))
            kH = [sb3(f"kH{s}", [128, GB, NH, N]) for s in range(S)]
            v = [sb3(f"v{s}", [128, GB, NH, HD + 1]) for s in range(S)]
            pr = [[sb3(f"pr{s}{b}", [128, NH, N]) for b in range(GB)] for s in range(S)]
            prT = [sb3(f"prT{k}", [128, NH, N]) for k in range(2)]
            mx = [sb3(f"mx{s}", [128, GB, NH]) for s in range(S)]
            rec = [sb3(f"rec{s}", [128, GB, NH]) for s in range(S)]
            in_s, out_s = ([sb3(f"{n}{s}", [128, GB, 6]) for s in range(S)] for n in ("in_s", "out_s"))
            in_mv, out_mv = ([sb3(f"{n}{s}", [128, GB, 2]) for s in range(S)] for n in ("in_mv", "out_mv"))
            in_r, out_r, out_mr, out_sh = ([sb3(f"{n}{s}", [128, GB]) for s in range(S)]
                                           for n in ("in_r", "out_r", "out_mr", "out_sh"))
            PTB = [tile[0], tile[1]]
            OB = [bank[6 + k][:, 0:2 * NH * (HD + 1)].rearrange("p (b h e) -> p b h e", b=2, h=NH) for k in range(2)]
            SB, ST = bank[2:6], tile[2:6]
            X3T_T, K_B, Q_B, V_B, Z_T = 3, 0, 1, 1, 2
            BN2_DONE = 1 + 5
            SCALE = float(1.0 / HD ** 0.5)

            def group3(it, s):
                return bass.ds(it * (S * GB) + s * GB, GB)

            def halves(slot):
                def body(it):
                    for s in range(S):
                        for b in range(GB):
                            slot(it, s, b)
                return body

            def graph(it, s, b, lag, piece):
                n = (b - lag) // GB
                each(it, s, n, piece, (b - lag) % GB)

            with nc.Block() as block:
                @block.sync
                def _(sp):
                    for s in range(S):
                        sp.sem_inc(out_done[s], 16)

                    def load(it, s):
                        sp.wait_ge(in_dve[s], IN_DVE.done_before(it, "y"))
                        settle(sp)
                        sp.dma_start(x2b[s][:], x2_dram[:, group3(it, s), :]).then_inc(x2_in[s], 16)

                    def store(it, s):
                        sp.wait_ge(out_act[s], OUT_ACT.done(it, "out"))
                        settle(sp)
                        sp.dma_start(out[:, group3(it, s), :], fin[s][:]).then_inc(out_done[s], 16)

                    def body(it):
                        for s in range(S):
                            each(it, s, 4, load)
                            each(it, s, -2, store)

                    over(sp, body, 2)
                    for s in range(S):
                        sp.wait_ge(out_done[s], 16 * NIT + 16)

                @block.gpsimd
                def _(pool):
                    for sems, steps in ((in_pool, IN_POOL), (att_pool, ATT_POOL), (out_pool, OUT_POOL)):
                        for s in range(S):
                            pool.sem_inc(sems[s], steps.total)
                    for s in range(S):
                        pool.memset(v[s][:, :, :, HD:HD + 1], 1.0).then_inc(fixed_set, 1)
                        pool.memset(kH[s][:], 0.0).then_inc(fixed_set, 1)
                    bn_pool(pool, bn2_dve, bn2_pool, 1, bn2_mv[:, 1:2], bn2_scale[:])

                    def rstd(r, mv, done, steps, it):
                        settle(pool)
                        pool.tensor_scalar(r[:], mv[:, :, 1], EPS, None, ALU.add).then_inc(done, 1)
                        pool.wait_ge(done, steps.done(it, "veps"))
                        pool.tensor_tensor(r[:], r[:], minus_half[:], ALU.pow).then_inc(done, 1)

                    def sub(it, s, b):
                        pool.wait_ge(att_dve[s], ATT_DVE.done(it, f"max{b}"))
                        pool.tensor_tensor(pr[s][b][:], pr[s][b][:], mx[s][:, b, :].unsqueeze(2).broadcast_to([128, NH, N]),
                                           ALU.subtract).then_inc(att_pool[s], 1)

                    def in_norm(it, s):
                        pool.wait_ge(in_dve[s], IN_DVE.done(it, "aggr"))
                        rstd(in_r[s], in_mv[s], in_pool[s], IN_POOL, it)

                    def residual(it, s):
                        pool.wait_ge(save_act[s], SAVE_ACT.done(it, "x3k"))
                        pool.wait_ge(out_dve[s], OUT_DVE.done(it, "att"))
                        pool.tensor_tensor(yc[s][:], yc[s][:], x3k[s][:], ALU.add).then_inc(out_pool[s], 1)

                    def last_norm(it, s):
                        pool.wait_ge(out_act[s], OUT_ACT.done_before(it, "out"))
                        pool.wait_ge(out_dve[s], OUT_DVE.done(it, "aggr"))
                        rstd(out_r[s], out_mv[s], out_pool[s], OUT_POOL, it)
                        pool.wait_ge(out_pool[s], OUT_POOL.done(it, "rstd"))
                        pool.tensor_tensor(out_mr[s][:], out_r[s][:], out_mv[s][:, :, 0], ALU.mult).then_inc(out_pool[s], 1)
                        pool.wait_ge(out_pool[s], OUT_POOL.done(it, "mr"))
                        settle(pool)
                        pool.tensor_scalar(out_sh[s][:], out_mr[s][:], -1.0, None, ALU.mult).then_inc(out_pool[s], 1)

                    def slot(it, s, b):
                        if b == 3:
                            each(it, s, -1, residual)
                        each(it, s, 0, sub, b)
                        if b == 0:
                            each(it, s, 2, in_norm)
                        if b == 1:
                            each(it, s, -2, last_norm)

                    over(pool, halves(slot), 2)

                @block.tensor
                def _(pe):
                    for sems, steps in ((in_pe, IN_PE), (qkv_pe, QKV_PE), (att_pe, ATT_PE)):
                        for s in range(S):
                            pe.sem_inc(sems[s], steps.total)

                    def turn_tile(dst, src):
                        for b in range(GB):
                            last = pe.transpose(dst[:, b, :], src[:, b, :], ident[:])
                        return last

                    def other(it, s, sems, steps, name):
                        if s:
                            pe.wait_ge(sems[0], steps.done(it, name))
                        else:
                            pe.wait_ge(sems[1], steps.done_before(it, name))

                    def zt(it, s):
                        other(it, s, in_dve, IN_DVE, "y")
                        if not isinstance(it, int) or S * it + s >= 3:
                            jt, js = shift(it, s, -3)
                            pe.wait_ge(att_dve[js], ATT_DVE.done(jt, "m2"))
                        pe.wait_ge(in_act[s], IN_ACT.done(it, "z"))
                        turn_tile(ST[Z_T], z[s]).then_inc(in_pe[s], 1)

                    def x3t(it, s):
                        pe.wait_ge(att_dve[s], ATT_DVE.done_before(it, "m3"))
                        other(it, s, qkv_act, QKV_ACT, "x3t")
                        pe.wait_ge(in_dve[s], IN_DVE.done(it, "x3"))
                        turn_tile(ST[X3T_T], x3[s]).then_inc(qkv_pe[s], 1)

                    def k(it, s):
                        other(it, s, att_dve, ATT_DVE, "m0")
                        pe.wait_ge(qkv_act[s], QKV_ACT.done(it, "x3t"))
                        pe.matmul(SB[K_B][:], w3[:, D:2 * D], flat(x3T[s][:]), start=True, stop=True).then_inc(qkv_pe[s], 1)

                    def q(it, s):
                        other(it, s, att_dve, ATT_DVE, "m1")
                        pe.matmul(SB[Q_B][:], w3[:, 0:D], flat(x3T[s][:]), start=True, stop=True).then_inc(qkv_pe[s], 1)

                    def vee(it, s):
                        pe.wait_ge(qkv_act[s], QKV_ACT.done(it, "q"))
                        for b in range(GB):
                            last = pe.matmul(ST[V_B][:, b, :], x3T[s][:, b, :], w3[:, 2 * D:3 * D], start=True, stop=True)
                        last.then_inc(qkv_pe[s], 1)

                    def scores(it, s, b):
                        if b == 0:
                            pe.wait_ge(qkv_act[s], QKV_ACT.done(it, "q"))
                        if b == 1:
                            pe.wait_ge(qkv_act[s], QKV_ACT.done(it, "v"))
                        if b == 2 and exists(it + 1):
                            pe.wait_ge(in_dve[s], IN_DVE.done(it + 1, "y"))
                        if b == 3:
                            jt, js = shift(it, s, 1)
                            if exists(jt):
                                pe.wait_ge(qkv_act[js], QKV_ACT.done(jt, "x3t"))
                            else:
                                other(it, s, att_dve, ATT_DVE, "m3")
                        pe.matmul(SB[b][:], qT[s][:, b, :], flat(kH[s][:, b]), start=True, stop=True).then_inc(att_pe[s], 1)

                    def turn(it, s, b):
                        if b < 2:
                            other(it, s, att_act, ATT_ACT, f"pt{b + 2}")
                        pe.wait_ge(att_act[s], ATT_ACT.done(it, f"exp{b}"))
                        turn_tile(PTB[b % 2], pr[s][b]).then_inc(att_pe[s], 1)

                    def values(it, s, b):
                        if b == 0:
                            other(it, s, out_dve, OUT_DVE, "att")
                            pe.wait_ge(qkv_act[s], QKV_ACT.done(it, "v"))
                        pe.wait_ge(att_act[s], ATT_ACT.done(it, f"pt{b}"))
                        for h in range(NH):
                            last = pe.matmul(OB[b // 2][:, b % 2, h, :], prT[b % 2][:, h, :], v[s][:, b, h, :],
                                             start=True, stop=True)
                        last.then_inc(att_pe[s], 1)

                    def slot(it, s, b):
                        if b == 0:
                            each(it, s, 0, scores, 0)
                        if b == 3:
                            each(it, s, 3, zt)
                        each(it, s, 1, (x3t, k, q, vee)[b])
                        graph(it, s, b, 2, turn)
                        if b < 3:
                            each(it, s, 0, scores, b + 1)
                        graph(it, s, b, 3, values)

                    pe.wait_ge(fixed_set, 2 * S)
                    over(pe, halves(slot), 2)

                @block.scalar
                def _(act):
                    for sems, steps in ((in_act, IN_ACT), (qkv_act, QKV_ACT), (att_act, ATT_ACT), (save_act, SAVE_ACT),
                                        (out_act, OUT_ACT)):
                        for s in range(S):
                            act.sem_inc(sems[s], steps.total)
                    act.wait_ge(bn2_dve, BN2_DONE)
                    act.wait_ge(fixed_set, 2 * S)

                    def norm(dst, src, r, sh):
                        for b in range(GB):
                            last = act.activation(dst[:, b, :], src[:, b, :], ACT.Identity, bias=sh[:, b:b + 1],
                                                  scale=r[:, b:b + 1])
                        return last

                    def batch_norm(it, s):
                        act.wait_ge(in_pe[s], IN_PE.done_before(it, "zt"))
                        settle(act)
                        act.activation(z[s][:], agg_all[:, group3(it, s), :], ACT.Identity, bias=bn2_shift[:, 0:1],
                                       scale=bn2_scale[:, 0:1]).then_inc(in_act[s], 1)

                    def keep(it, s):
                        act.wait_ge(out_pool[s], OUT_POOL.done_before(it, "y"))
                        act.wait_ge(in_dve[s], IN_DVE.done(it, "x3"))
                        act.activation(x3k[s][:], x3[s][:], ACT.Copy).then_inc(save_act[s], 1)

                    def copy(it, s, name, dst, src):
                        act.wait_ge(qkv_pe[s], QKV_PE.done(it, name))
                        act.activation(dst, src, ACT.Copy).then_inc(qkv_act[s], 1)

                    def x3t(it, s):
                        copy(it, s, "x3t", x3T[s][:], ST[X3T_T])

                    def k(it, s):
                        act.wait_ge(qkv_pe[s], QKV_PE.done(it, "k"))
                        for h in range(NH):
                            rows = slice(h * HD, (h + 1) * HD)
                            last = act.activation(kH[s][rows, :, h, :], ST[K_B][rows], ACT.Copy)
                        last.then_inc(qkv_act[s], 1)

                    def q(it, s):
                        copy(it, s, "q", qT[s][:], ST[Q_B])

                    def vee(it, s):
                        copy(it, s, "v", v[s][:, :, :, 0:HD], ST[V_B].rearrange("p b (h e) -> p b h e", h=NH))

                    def exp(it, s, b):
                        act.wait_ge(att_pool[s], ATT_POOL.done(it, f"sub{b}"))
                        act.activation(pr[s][b][:], pr[s][b][:], ACT.Exp).then_inc(att_act[s], 1)

                    def turned(it, s, b):
                        act.wait_ge(att_pe[s], ATT_PE.done(it, f"pt{b}"))
                        act.activation(prT[b % 2][:], PTB[b % 2], ACT.Copy).then_inc(att_act[s], 1)

                    def last_norm(it, s):
                        act.wait_ge(out_pool[s], OUT_POOL.done(it, "shift"))
                        act.wait_ge(out_done[s], it * 16 + 16)
                        settle(act)
                        norm(fin[s], yc[s], out_r[s], out_sh[s]).then_inc(out_act[s], 1)

                    def slot(it, s, b):
                        graph(it, s, b, 1, exp)
                        each(it, s, 1, (x3t, k, q, vee)[b])
                        graph(it, s, b, 2, turned)
                        if b == 0:
                            each(it, s, 3, batch_norm)
                            each(it, s, 0, keep)
                        if b == 3:
                            each(it, s, -2, last_norm)

                    over(act, halves(slot), 2)

                @block.vector
                def _(dve):
                    for sems, steps in ((in_dve, IN_DVE), (att_dve, ATT_DVE), (out_dve, OUT_DVE)):
                        for s in range(S):
                            dve.sem_inc(sems[s], steps.total)
                    n = bn_dve(dve, bn2_dve, bn2_pool, 1, [bn2_stats[:].rearrange("p a b -> p (a b)")], [bn2_mv[:]],
                               bn2_par[:, 0:1], bn2_par[:, 1:2], bn2_par[:, 2:3], bn2_scale[:], bn2_shift[:])
                    assert n == BN2_DONE

                    def norm_stats(it, y, st, mv, done, steps):
                        settle(dve)
                        for b in range(GB):
                            last = dve.bn_stats(st[:, b, :], y[:, b, :])
                        last.then_inc(done, 1)
                        dve.wait_ge(done, steps.done(it, "stats"))
                        settle(dve)
                        for b in range(GB):
                            last = dve.bn_aggr(mv[:, b, :], st[:, b, :])
                        last.then_inc(done, 1)

                    def residual(it, s):
                        dve.wait_ge(x2_in[s], it * 16 + 16)
                        dve.wait_ge(in_pe[s], IN_PE.done(it, "zt"))
                        dve.tensor_tensor(ya[s][:], ST[Z_T], x2b[s][:], ALU.add).then_inc(in_dve[s], 1)

                    def in_stats(it, s):
                        dve.wait_ge(in_dve[s], IN_DVE.done(it, "y"))
                        norm_stats(it, ya[s], in_s[s], in_mv[s], in_dve[s], IN_DVE)

                    def in_norm(it, s):
                        dve.wait_ge(save_act[s], SAVE_ACT.done_before(it, "x3k"))
                        dve.wait_ge(qkv_pe[s], QKV_PE.done_before(it, "x3t"))
                        dve.wait_ge(in_pool[s], IN_POOL.done(it, "rstd"))
                        settle(dve)
                        for b in range(GB):
                            last = dve.tensor_scalar(x3[s][:, b, :], ya[s][:, b, :], in_mv[s][:, b, 0:1],
                                                     in_r[s][:, b:b + 1], ALU.subtract, ALU.mult)
                        last.then_inc(in_dve[s], 1)

                    def mask_max(it, s, b):
                        dve.wait_ge(att_pe[s], ATT_PE.done(it, f"sc{b}"))
                        dve.scalar_tensor_tensor(pr[s][b][:], ST[b], SCALE, mask[:].unsqueeze(1).broadcast_to([128, NH, N]),
                                                 ALU.mult, ALU.add).then_inc(att_dve[s], 1)
                        dve.wait_ge(att_dve[s], ATT_DVE.done(it, f"m{b}"))
                        dve.reduce_max(mx[s][:, b, :], pr[s][b][:], AX).then_inc(att_dve[s], 1)

                    def over_sums(it, s):
                        dve.wait_ge(att_pe[s], ATT_PE.done(it, "pv3"))
                        settle(dve)
                        for k in range(2):
                            last = dve.reciprocal(rec[s][:, 2 * k:2 * k + 2, :], OB[k][:, :, :, HD])
                        last.then_inc(out_dve[s], 1)
                        dve.wait_ge(out_dve[s], OUT_DVE.done(it, "rec"))
                        dve.wait_ge(out_act[s], OUT_ACT.done_before(it, "out"))
                        for k in range(2):
                            last = dve.tensor_tensor(
                                yc[s][:, 2 * k:2 * k + 2, :].rearrange("p b (h e) -> p b h e", h=NH), OB[k][:, :, :, 0:HD],
                                rec[s][:, 2 * k:2 * k + 2, :].unsqueeze(3).broadcast_to([128, 2, NH, HD]), ALU.mult)
                        last.then_inc(out_dve[s], 1)

                    def out_stats(it, s):
                        dve.wait_ge(out_pool[s], OUT_POOL.done(it, "y"))
                        norm_stats(it, yc[s], out_s[s], out_mv[s], out_dve[s], OUT_DVE)

                    def slot(it, s, b):
                        each(it, s, 0, mask_max, b)
                        if b == 3:
                            each(it, s, 3, residual)
                        if b == 0:
                            each(it, s, 2, in_stats)
                        if b == 1:
                            each(it, s, -2, out_stats)
                        if b == 2:
                            each(it, s, -1, over_sums)
                            each(it, s, 2, in_norm)

                    over(dve, halves(slot), 2)


def kernel(**inputs):
    import numpy as np
    import concourse.bacc as _bacc
    from concourse.bass_utils import run_bass_kernel_spmd as _run

    a = {k: np.asarray(v) for k, v in inputs.items()}
    l0, l1, l2 = "L0_gnn_", "L1_gnn_", "L2_gnn_"

    def gates_last(b):
        return b.reshape(MAXW, 4, 128).transpose(2, 0, 1).reshape(128, MAXW * 4)

    lay = {
        "x_t": a["x"].transpose(1, 0, 2), "x_f": a["x"].transpose(2, 0, 1),
        "adj": a["adj"], "adjT": a["adj"].T,
        "eb": a[l0 + "edge_bias"], "oeb": a[l0 + "out_edge_bias"],
        "gate_w": np.concatenate([a[l0 + "gate_weight"], a[l0 + "out_gate_weight"], a[l0 + "loop_gate"]], 1),
        "gate_b": np.concatenate([a[l0 + "bias_gate"], a[l0 + "out_bias_gate"]], 1),
        "wg0": a[l1 + "Wg0"], "wg1": a[l1 + "Wg1"], "bg0": a[l1 + "bg0"], "bg1": a[l1 + "bg1"],
        "wihT": a[l1 + "Wih"].transpose(2, 0, 1), "whhT": a[l1 + "Whh"].transpose(2, 0, 1),
        "bih": gates_last(a[l1 + "bih"]), "bhh": gates_last(a[l1 + "bhh"]),
        "w1T": a[l2 + "W1"].T, "w2T": a[l2 + "W2"].T.reshape(H1, 128, D).transpose(1, 0, 2),
        "bn1": np.stack([a[l2 + n].reshape(H1, 128).T for n in ("b1", "g1", "be1")], 1),
        "bn2": np.stack([a[l2 + n] for n in ("b2", "g2", "be2")], 1),
        "w3": a["L3_gnn_W"],
    }
    nc = _bacc.Bacc("TRN2", target_bir_lowering=False, num_devices=1)
    arrays = {f"in_{k}": np.ascontiguousarray(v) for k, v in lay.items()}
    t = {k: nc.dram_tensor(f"in_{k}", arrays[f"in_{k}"].shape, F32, kind="ExternalInput").ap() for k in lay}
    out = nc.dram_tensor("out_dram", (N, B, D), F32, kind="ExternalOutput").ap()
    build(nc, t, out)
    r = _run(nc, [arrays], core_ids=[0])
    return np.ascontiguousarray(r.results[0]["out_dram"].transpose(1, 0, 2))
```
